# Optimizing a Trainium2 kernel written in Bass

```python
import numpy as np
import jax
import jax.numpy as jnp

def _softmax(x, axis=-1):
    return jax.nn.softmax(x, axis=axis)

def _gelu(x):
    return jax.nn.gelu(x, approximate=True)

def _silu(x):
    return jax.nn.silu(x)

def _sigmoid(x):
    return jax.nn.sigmoid(x)

def _layernorm(x, axis=-1, eps=1e-05):
    m = jnp.mean(x, axis=axis, keepdims=True)
    v = jnp.var(x, axis=axis, keepdims=True)
    return (x - m) / jnp.sqrt(v + eps)

def _scatter_add(tgt, idx, src, axis=0):
    return tgt.at[idx].add(src)

def _segment_sum(src, seg, n):
    return jax.ops.segment_sum(src, seg, n)
kernel_name = 'mk_prb_d1_jaxref_r8_34a4c9'

def setup_inputs(seed: int=0):
    np.random.seed(seed)
    _w = jnp.asarray

    def _L0_attn_setup():
        import jax, jax.numpy as jnp
        import numpy as np
        NUM_HEADS = 16
        HEAD_SIZE = 128

        def _alibi_mask(seq_len: int, num_heads: int) -> jnp.ndarray:
            if num_heads <= 8:
                slopes = jnp.asarray([1.0 / 2.0 ** i for i in range(num_heads)], dtype=jnp.float32)
            else:
                slopes = jnp.asarray([1.0 / 2.0 ** (i / 2.0) for i in range(num_heads)], dtype=jnp.float32)
            i = jnp.arange(seq_len)[:, None]
            j = jnp.arange(seq_len)[None, :]
            base = jnp.where(j <= i, -(i - j).astype(jnp.float32), -jnp.inf)
            return slopes[:, None, None] * base
        key = jax.random.key(seed)
        ks = jax.random.split(key, 5)
        H = 256
        s = 0.02
        return {'x': jax.random.normal(ks[0], (2, 256, H), dtype=jnp.float32), 'qkv_w': jax.random.normal(ks[1], (H, 3 * NUM_HEADS * HEAD_SIZE), dtype=jnp.float32) * s, 'qkv_b': jax.random.normal(ks[2], (3 * NUM_HEADS * HEAD_SIZE,), dtype=jnp.float32) * s, 'out_w': jax.random.normal(ks[3], (NUM_HEADS * HEAD_SIZE, H), dtype=jnp.float32) * s, 'out_b': jax.random.normal(ks[4], (H,), dtype=jnp.float32) * s}
    _L0_attn_in = _L0_attn_setup()

    def _L0_ffn_setup():
        import jax, jax.numpy as jnp
        import numpy as np
        HIDDEN = 256
        INTER = 688
        LUT_SIZE = 16

        def _ghost_linear(x, idx, lut):
            w = lut[idx]
            return jnp.einsum('bsh,oh->bso', x, w)
        key = jax.random.key(seed)
        k_x, k_lut, k_g, k_u, k_d = jax.random.split(key, 5)
        x = jax.random.normal(k_x, (2, 512, HIDDEN), dtype=jnp.float32)
        lut = jax.random.normal(k_lut, (LUT_SIZE,), dtype=jnp.float32) * 0.02
        gate_idx = jax.random.randint(k_g, (INTER, HIDDEN), 0, LUT_SIZE, dtype=jnp.int32)
        up_idx = jax.random.randint(k_u, (INTER, HIDDEN), 0, LUT_SIZE, dtype=jnp.int32)
        down_idx = jax.random.randint(k_d, (HIDDEN, INTER), 0, LUT_SIZE, dtype=jnp.int32)
        return {'x': x, 'lut': lut, 'gate_idx': gate_idx, 'up_idx': up_idx, 'down_idx': down_idx}
    _L0_ffn_in = _L0_ffn_setup()
    _d = {'L0_attn_x': _L0_attn_in['x'], 'L0_attn_qkv_w': _L0_attn_in['qkv_w'], 'L0_attn_qkv_b': _L0_attn_in['qkv_b'], 'L0_attn_out_w': _L0_attn_in['out_w'], 'L0_attn_out_b': _L0_attn_in['out_b'], 'L0_ffn_lut': _L0_ffn_in['lut'], 'L0_ffn_gate_idx': _L0_ffn_in['gate_idx'], 'L0_ffn_up_idx': _L0_ffn_in['up_idx'], 'L0_ffn_down_idx': _L0_ffn_in['down_idx']}
    _x0 = _d['L0_attn_x']
    _d['L0_attn_x'] = jax.random.normal(jax.random.fold_in(jax.random.key(seed), 1), (1, 1024, 256), dtype=_x0.dtype)
    del _x0
    return _d

def reference(L0_attn_x, L0_attn_qkv_w, L0_attn_qkv_b, L0_attn_out_w, L0_attn_out_b, L0_ffn_lut, L0_ffn_gate_idx, L0_ffn_up_idx, L0_ffn_down_idx):

    def _L0_attn_ref(x, qkv_w, qkv_b, out_w, out_b):
        import jax, jax.numpy as jnp
        import numpy as np
        NUM_HEADS = 16
        HEAD_SIZE = 128

        def _alibi_mask(seq_len: int, num_heads: int) -> jnp.ndarray:
            if num_heads <= 8:
                slopes = jnp.asarray([1.0 / 2.0 ** i for i in range(num_heads)], dtype=jnp.float32)
            else:
                slopes = jnp.asarray([1.0 / 2.0 ** (i / 2.0) for i in range(num_heads)], dtype=jnp.float32)
            i = jnp.arange(seq_len)[:, None]
            j = jnp.arange(seq_len)[None, :]
            base = jnp.where(j <= i, -(i - j).astype(jnp.float32), -jnp.inf)
            return slopes[:, None, None] * base
        b, s, h = x.shape
        qkv = x @ qkv_w + qkv_b
        q, k, v = jnp.split(qkv, 3, axis=-1)

        def to_heads(t):
            return t.reshape(b, s, NUM_HEADS, HEAD_SIZE).transpose(0, 2, 1, 3)
        q, k, v = (to_heads(q), to_heads(k), to_heads(v))
        scores = jnp.einsum('bhid,bhjd->bhij', q, k) + _alibi_mask(s, NUM_HEADS)[None]
        attn = jax.nn.softmax(scores, axis=-1)
        ctx = jnp.einsum('bhij,bhjd->bhid', attn, v)
        ctx = ctx.transpose(0, 2, 1, 3).reshape(b, s, NUM_HEADS * HEAD_SIZE)
        return ctx @ out_w + out_b

    def _L0_ffn_ref(x, lut, gate_idx, up_idx, down_idx):
        import jax, jax.numpy as jnp
        import numpy as np
        HIDDEN = 256
        INTER = 688
        LUT_SIZE = 16

        def _ghost_linear(x, idx, lut):
            w = lut[idx]
            return jnp.einsum('bsh,oh->bso', x, w)
        gate = _ghost_linear(x, gate_idx, lut)
        up = _ghost_linear(x, up_idx, lut)
        h = jax.nn.silu(gate) * up
        return _ghost_linear(h, down_idx, lut)
    x = L0_attn_x
    xn = _layernorm(x, axis=-1)
    x = x + _L0_attn_ref(xn, L0_attn_qkv_w, L0_attn_qkv_b, L0_attn_out_w, L0_attn_out_b) + _L0_ffn_ref(xn, L0_ffn_lut, L0_ffn_gate_idx, L0_ffn_up_idx, L0_ffn_down_idx)
    return x

_drawn_inputs = setup_inputs


def setup_inputs(seed=0):
    import zlib

    import numpy as np

    out = dict(_drawn_inputs(seed))
    spreads = {}
    factors = {'L0_attn_qkv_b': 2.88, 'L0_attn_out_b': 2.934}
    for name, (base, spread) in spreads.items():
        noise = np.random.default_rng([zlib.crc32(name.encode()), seed]).standard_normal(out[name].shape)
        drawn = base * np.exp(spread * noise) if base else spread * noise
        out[name] = jnp.asarray(drawn.astype(out[name].dtype))
    for name, factor in factors.items():
        out[name] = (out[name] * factor).astype(out[name].dtype)
    return out
```

```python
from contextlib import ExitStack

import concourse.bass as bass
from concourse import mybir

ALU = mybir.AluOpType
ACT = mybir.ActivationFunctionType
F32 = mybir.dt.float32
F32R = mybir.dt.float32r
I32 = mybir.dt.int32
U8 = mybir.dt.uint8

P = 128
S, HID, HEADS, D = 1024, 256, 16, 128
INTER, LUT = 688, 16
EPS = 1e-5
KT = HID // P
NT = S // P
HALF = 512
PAIRS = HEADS // 2
FT = -(-INTER // P)
MASKED = -1.0e38
LAG = 2

GROUPS = [-(-(i + 1) // 4) for i in range(NT)]
GROUPS_BEFORE = [sum(GROUPS[:i]) for i in range(NT + 1)]
HEAD_GROUPS = GROUPS_BEFORE[NT]

SLOT_W = [(i + 5) * P for i in range(4)]
SLOT_AT = [sum(SLOT_W[:i]) for i in range(4)]

PT_TIGHT, PT_ROW = 384, HALF
PT_HALF0 = 3 * PT_TIGHT + HALF
PT_WIDE = 2 * PT_HALF0
PT_COLS = PT_WIDE + 4 * PT_ROW

PIECE = 4 * P
PIECES = FT + FT * HID // PIECE
WF = PIECES * PIECE
LUT_PIECE = WF // NT


def pt_at(half, j):
    if half == 0:
        return PT_HALF0 + j * PT_TIGHT
    return PT_WIDE + j * PT_ROW if j < 4 else (j - 4) * PT_TIGHT


def pt_from(half, j):
    return min(max(0, j - 4 * half) * P, 2 * P)


UNITS = [
    (("_out0", 0), ("q1", 0), ("_out1", 1), ("k1", 1), ("nq0", 2), ("nk0", 2), ("_pv1", 3),
     ("v0", 4), ("v1", 4), ("_out2", 5), ("v2", 5), ("pv0", 6), ("v3", 6), ("_out3", 7)),
    (("q1", 0), ("k1", 1), ("_pv1", 3), ("nq0", 5), ("pv0", 6), ("nk0", 6)),
]
FIRST, STEADY, LAST = "first", "steady", "last"


def units_of(kind, p):
    return [(name, step) for name, step in UNITS[p]
            if not (kind == FIRST and p == 0 and name[0] == "_") and not (kind == LAST and p == 1 and name[0] == "n")]


def is_split(name):
    return "out" not in name


def counted(kind, only):
    return [(p, name) for p in range(2) for name, _ in units_of(kind, p) if only(name)]


def number(n, kind, p, name, only=lambda name: True):
    here = counted(kind, only).index((p, name)) + 1
    per = len(counted(STEADY, only))
    return n * per + 2 + here - (0 if kind == FIRST else per - len(counted(FIRST, only)))


def bank_of(kind, p, name):
    return (number(0 if kind == FIRST else 2, kind, p, name) - 1) % 2


def block_ffn(nc, x, w_qk, w_v, w_o, b_qkv, b_out, lut, idx, out):
    with ExitStack() as ctx:
        def sb(name, shape, dt=F32):
            return ctx.enter_context(nc.sbuf_tensor(name, shape, dt))

        def sem(name):
            return ctx.enter_context(nc.semaphore(name))

        acc = sb("acc", [P, NT, HID])
        work = sb("work", [P, sum(SLOT_W)])
        xn_t = [sb(f"xn_t_{s}", [P, KT, S], F32R) for s in ("hi", "lo")]
        qk = [sb(f"qk_{s}", [P, 2, 2, S], F32R) for s in ("hi", "lo")]
        v = [sb(f"v_{s}", [P, NT, 2 * D], F32R) for s in ("hi", "lo")]
        p_t = [sb(f"p_t_{s}", [P, PT_COLS], F32R) for s in ("hi", "lo")]
        ctx_t = [sb(f"ctx_t_{s}", [P, 2, S], F32R) for s in ("hi", "lo")]
        qk_raw = sb("qk_raw", [P, KT, 2 * D])
        qk_w = [sb(f"qk_w_{s}", [P, 2, KT, 2 * D], F32R) for s in ("hi", "lo")]
        v_raw = sb("v_raw", [P, KT, 2 * D])
        v_w = [sb(f"v_w_{s}", [P, KT, 2 * D], F32R) for s in ("hi", "lo")]
        o_raw = sb("o_raw", [P, 2, HID])
        o_w = [sb(f"o_w_{s}", [P, 2, HID], F32R) for s in ("hi", "lo")]
        distance = sb("distance", [P, S])
        alibi = sb("alibi", [P, 2, S])
        codes = sb("codes", [P, WF], U8)
        w_ffn = sb("w_ffn", [P, WF])
        term = sb("term", [P, 2, LUT_PIECE])
        ident = sb("ident", [P, P])
        bias = sb("bias", [P, HEADS, 3])
        bias_now = sb("bias_now", [P, 2, 3])
        table = sb("table", [P, LUT])
        entry = sb("entry", [P, LUT])
        slope = sb("slope", [P, HEADS])
        pad = sb("pad", [P, 4 * NT])
        neg_max = sb("neg_max", [P, 2 * NT])
        row_sum = sb("row_sum", [P, 2 * NT])
        inv_sum = sb("inv_sum", [P, 2 * NT])
        stats = sb("stats", [P, NT, 6])
        moments = sb("moments", [P, NT, 2])
        ln = sb("ln", [P, 4, NT])

        ps_s = ctx.enter_context(nc.psum_tensor("ps_s", [P, 2, S], F32))
        ps_t = ctx.enter_context(nc.psum_tensor("ps_t", [P, 2, HALF], F32))
        ps_u = ctx.enter_context(nc.psum_tensor("ps_u", [P, 2, HALF], F32))

        x_landed, bias_landed, small_landed = [sem("x0_landed"), sem("x1_landed")], sem("bias_landed"), sem("small_landed")
        idx_landed, qk_landed = sem("idx_landed"), sem("qk_landed")
        v_landed, o_landed, stored = sem("v_landed"), sem("o_landed"), sem("stored")
        xn_turned, scores_done, p_turned = sem("xn_turned"), sem("scores_done"), sem("p_turned")
        unit_done, gate_up_done, down_done = sem("unit_done"), sem("gate_up_done"), sem("down_done")
        root_done, xn_hi, exp_done, p_hi = sem("root_done"), sem("xn_hi"), sem("exp_done"), sem("p_hi")
        unit_hi, qk_w_hi, v_w_hi, o_w_hi = sem("unit_hi"), sem("qk_w_hi"), sem("v_w_hi"), sem("o_w_hi")
        ffn_w_hi, silu_done, h_hi_done = sem("ffn_w_hi"), sem("silu_done"), sem("h_hi_done")
        ln_step, xn_ready, xn_lo = sem("ln_step"), sem("xn_ready"), sem("xn_lo")
        bias_ready = sem("bias_ready")
        cleared, codes_ready, alibi_ready = sem("cleared"), sem("codes_ready"), sem("alibi_ready")
        scores_masked, inv_ready, p_lo = sem("scores_masked"), sem("inv_ready"), sem("p_lo")
        unit_used, term_ready = sem("unit_used"), sem("term_ready")
        h_ready, h_lo_done, out_ready = sem("h_ready"), sem("h_lo_done"), sem("out_ready")
        iota_done, made, normed, term_added = sem("iota_done"), sem("made"), sem("normed"), sem("term_added")
        qk_w_lo, v_w_lo, o_w_lo, ffn_w_lo = sem("qk_w_lo"), sem("v_w_lo"), sem("o_w_lo"), sem("ffn_w_lo")

        block = ctx.enter_context(nc.Block())

        xn = work[:, 0:NT * HID].rearrange("p (t h) -> p t h", t=NT)

        def slot(i, width=None):
            at = SLOT_AT[i % 4]
            return work[:, at:at + (width or (i + 1) * P)]

        def turned(i, g):
            return range(4 * g, min(4 * g + 4, i + 1))

        def p_rows(part, i, g):
            half, js = i // 4, turned(i, g)
            at, step = pt_at(half, js[0]), (PT_ROW if half and g == 0 else PT_TIGHT)
            q = (i % 4) * P
            if step == PT_ROW:
                rows = p_t[part][:, at:at + 4 * step].rearrange("p (j q) -> p j q", q=step)
                return rows[:, 0:len(js), q:q + P]
            rows = p_t[part][:, at + q:at + q + len(js) * step].rearrange("p (j q) -> p j q", q=step)
            return rows[:, :, 0:P]

        def tile_no(n, p, i):
            return n * (2 * NT) + p * NT + i

        def groups_to(n, p, i):
            if i < 0:
                return n * (2 * HEAD_GROUPS) + (p - 1) * HEAD_GROUPS + GROUPS_BEFORE[i + NT + 1]
            return n * (2 * HEAD_GROUPS) + p * HEAD_GROUPS + GROUPS_BEFORE[i + 1]

        def lagged(kind, p, i):
            if i >= LAG:
                return i - LAG
            return None if kind == FIRST and p == 0 else i - LAG + NT

        def parity_of(p, name):
            return 1 - p if name[0] in "n_" else p

        def unit_place(part, p, name):
            pr, c = parity_of(p, name), int(name[-1])
            if "q" in name or "k" in name:
                return qk[part][:, pr, int("k" in name), c * HALF:(c + 1) * HALF]
            if "pv" in name:
                return ctx_t[part][:, pr, c * HALF:(c + 1) * HALF]
            return v[part][:, 2 * c:2 * c + 2, :].rearrange("p t d -> p (t d)")

        def unit_bias(p, name):
            if "pv" not in name and "v" in name:
                return None
            which = 2 if "pv" in name else int("k" in name)
            return bias_now[:, parity_of(p, name), which:which + 1]

        def column(tensor, n, p):
            if isinstance(n, int):
                return tensor[:, 2 * n + p:2 * n + p + 1]
            return tensor[:, bass.ds(2 * n + p, 1)]

        def ffn_w(part, at, width=P):
            return p_t[part][:, at:at + width]

        def h_tile(part, u):
            if u < 8:
                return qk[part][:, :, :, :].rearrange("p a b s -> p (a b s)")[:, u * HALF:(u + 1) * HALF]
            return v[part][:, :, :].rearrange("p t d -> p (t d)")[:, (u - 8) * HALF:(u - 7) * HALF]

        def all_pairs(engine, pair):
            pair(0, FIRST)
            with engine.Fori(1, PAIRS - 1) as n:
                pair(n, STEADY)
            pair(PAIRS - 1, LAST)

        @block.sync
        def _(sp):
            x_t = x.rearrange("(t p) h -> p t h", p=P)
            for c in range(2):
                sp.dma_start(acc[:, 4 * c:4 * c + 4, :], x_t[:, 4 * c:4 * c + 4, :]).then_inc(x_landed[c], 16)
            sp.dma_start(qk_raw[:, :, :], w_qk[0]).then_inc(qk_landed, 16)
            sp.dma_start(bias[:, :, :], b_qkv).then_inc(bias_landed, 16)
            sp.dma_start(v_raw[:, :, :], w_v[0]).then_inc(v_landed, 16)
            sp.dma_start(table[:, :], lut.partition_broadcast(P)).then_inc(small_landed, 16)
            sp.dma_start(term[:, 0, 0:HID], b_out.partition_broadcast(P)).then_inc(small_landed, 16)
            sp.dma_start(w_ffn[:, :].bitcast(I32), idx).then_inc(idx_landed, 16)
            sp.dma_start(o_raw[:, :, :], w_o[0]).then_inc(o_landed, 16)
            for h in (1, 2):
                sp.wait_ge(qk_w_hi, h)
                sp.wait_ge(qk_w_lo, h)
                sp.dma_start(qk_raw[:, :, :], w_qk[h]).then_inc(qk_landed, 16)
            sp.wait_ge(v_w_hi, 1)
            sp.wait_ge(v_w_lo, 1)
            sp.dma_start(v_raw[:, :, :], w_v[1]).then_inc(v_landed, 16)

            def refill(n, to_the_end):
                sp.wait_ge(qk_w_hi, n * 2 + 3)
                sp.wait_ge(qk_w_lo, n * 2 + 3)
                sp.dma_start(qk_raw[:, :, :], w_qk[n * 2 + 3]).then_inc(qk_landed, 16)
                sp.wait_ge(o_w_hi, n + 1)
                sp.wait_ge(o_w_lo, n + 1)
                sp.dma_start(o_raw[:, :, :], w_o[n + 1]).then_inc(o_landed, 16)
                if to_the_end:
                    return
                sp.wait_ge(qk_w_hi, n * 2 + 4)
                sp.wait_ge(qk_w_lo, n * 2 + 4)
                sp.dma_start(qk_raw[:, :, :], w_qk[n * 2 + 4]).then_inc(qk_landed, 16)
                sp.wait_ge(v_w_hi, n + 2)
                sp.wait_ge(v_w_lo, n + 2)
                sp.dma_start(v_raw[:, :, :], w_v[n + 2]).then_inc(v_landed, 16)

            with sp.Fori(0, PAIRS - 2) as n:
                refill(n, False)
            refill(PAIRS - 2, True)
            out_t = out.rearrange("(t p) h -> p t h", p=P)
            for d in range(NT // 2):
                sp.wait_ge(out_ready, d + 1)
                sp.dma_start(out_t[:, 2 * d:2 * d + 2, :], acc[:, 2 * d:2 * d + 2, :]).then_inc(stored, 16)
            sp.wait_ge(stored, 16 * (NT // 2))

        @block.tensor
        def _(pe):
            def three(out, lhs, rhs, first, last):
                pe.matmul(out, lhs[0], rhs[0], start=first, stop=False)
                pe.matmul(out, lhs[0], rhs[1], start=False, stop=False)
                return pe.matmul(out, lhs[1], rhs[0], start=False, stop=last)

            def both(tensor, *where):
                return [t[where] for t in tensor]

            def free_bank(no):
                if isinstance(no, int) and no <= 2:
                    return
                pe.wait_ge(unit_used, no - 2)

            def project(bank, which, pr, c):
                for kk in range(KT):
                    last = three(ps_u[:, bank, :],
                                 both(qk_w, slice(None), pr, kk, slice(which * D, which * D + D)),
                                 both(xn_t, slice(None), kk, slice(c * HALF, c * HALF + HALF)),
                                 kk == 0, kk == KT - 1)
                last.then_inc(unit_done, 1)

            def values(bank, c):
                for t in (2 * c, 2 * c + 1):
                    for kk in range(KT):
                        last = three(ps_u[:, bank, (t % 2) * 2 * D:(t % 2 + 1) * 2 * D],
                                     both(xn_t, slice(None), kk, slice(t * P, t * P + P)),
                                     both(v_w, slice(None), kk, slice(None)),
                                     kk == 0, kk == KT - 1)
                last.then_inc(unit_done, 1)

            def context(bank, pr, c):
                tiles = 4 * c + 4
                for j in range(tiles):
                    q, at = pt_from(c, j), pt_at(c, j)
                    last = three(ps_u[:, bank, q:HALF],
                                 both(v, slice(None), j, slice(pr * D, pr * D + D)),
                                 both(p_t, slice(None), slice(at + q, at + HALF)),
                                 j == 0, j == tiles - 1)
                last.then_inc(unit_done, 1)

            def project_out(bank, c):
                for t in (2 * c, 2 * c + 1):
                    for pr in range(2):
                        last = three(ps_u[:, bank, (t % 2) * HID:(t % 2 + 1) * HID],
                                     both(ctx_t, slice(None), pr, slice(t * P, t * P + P)),
                                     both(o_w, slice(None), pr, slice(None)),
                                     pr == 0, pr == 1)
                last.then_inc(unit_done, 1)

            def unit(n, kind, p, name):
                bank, c = bank_of(kind, p, name), int(name[-1])
                free_bank(number(n, kind, p, name))
                if "q" in name or "k" in name:
                    if name in ("q1", "nq0"):
                        head = 2 * n + p + (name[0] == "n")
                        pe.wait_ge(qk_w_hi, head + 1)
                        pe.wait_ge(qk_w_lo, head + 1)
                    if name == "q1" and kind == FIRST and p == 0:
                        pe.wait_ge(xn_lo, 4)
                    project(bank, int("k" in name), parity_of(p, name), c)
                elif "pv" in name:
                    pe.wait_ge(p_lo, groups_to(n, p, 3 if c == 0 else -1))
                    if p == 0 and c == 0:
                        pe.wait_ge(unit_used, number(n, kind, 0, "v1"))
                    if p == 1 and c == 1:
                        pe.wait_ge(unit_used, number(n, kind, 0, "v3"))
                    context(bank, parity_of(p, name), c)
                elif "v" in name:
                    if c == 0:
                        pe.wait_ge(v_w_hi, n + 1)
                        pe.wait_ge(v_w_lo, n + 1)
                    values(bank, c)
                else:
                    if c == 0:
                        pe.wait_ge(o_w_hi, n)
                        pe.wait_ge(o_w_lo, n)
                        pe.wait_ge(unit_used, number(n, kind, 0, "_out0") - 2)
                    if c == 2:
                        pe.wait_ge(unit_used, number(n, kind, 0, "_pv1"))
                    project_out(bank, c)

            def scores(n, kind, p, i):
                if not (kind == FIRST and p == 0 and i < 2):
                    pe.wait_ge(scores_masked, tile_no(n, p, i) - 1)
                if i in (0, 4):
                    if i == 4:
                        pe.wait_ge(unit_used, number(n, kind, p, "k1"))
                    elif p == 1:
                        pe.wait_ge(unit_used, number(n, kind, 0, "nk0"))
                    elif kind == FIRST:
                        pe.wait_ge(unit_used, 2)
                        pe.wait_ge(xn_lo, 4)
                    else:
                        pe.wait_ge(unit_used, number(n, kind, 0, "_out0") - 1)
                width = (i + 1) * P
                for at in range(0, width, HALF):
                    to = max(min(width, at + HALF), at + 2 * P)
                    last = three(ps_s[:, i % 2, at:to],
                                 both(qk, slice(None), p, 0, slice(i * P, i * P + P)),
                                 both(qk, slice(None), p, 1, slice(at, to)), True, True)
                last.then_inc(scores_done, 1)

            def turn(n, p, i, back):
                pe.wait_ge(normed, tile_no(n, p, i - NT if back else i) + 1)
                for g in range(GROUPS[i]):
                    room = (GROUPS_BEFORE[i] + g) % 2
                    no = groups_to(n, p, i - NT - 1 if back else i - 1) + g + 1
                    if not (isinstance(no, int) and no <= 2):
                        pe.wait_ge(p_lo, no - 2)
                    for b, j in enumerate(turned(i, g)):
                        last = pe.transpose(ps_t[:, room, b * P:(b + 1) * P],
                                            slot(i)[:, j * P:(j + 1) * P], ident[:, :])
                    last.then_inc(p_turned, 1)

            pe.wait_ge(made, 2)
            for c in range(2):
                pe.wait_ge(xn_ready, 4 * c + 4)
                for kk in range(KT):
                    for t in range(4 * c, 4 * c + 4):
                        last = pe.transpose(ps_s[:, kk, t * P:(t + 1) * P], xn[:, t, kk * P:(kk + 1) * P],
                                            ident[:, :])
                    last.then_inc(xn_turned, 1)
            pe.wait_ge(xn_lo, 2)
            pe.wait_ge(qk_w_hi, 1)
            pe.wait_ge(qk_w_lo, 1)
            project(0, 0, 0, 0)
            project(1, 1, 0, 0)

            def pair(n, kind):
                for p in range(2):
                    for i in range(NT):
                        scores(n, kind, p, i)
                        for name, step in units_of(kind, p):
                            if step == i:
                                unit(n, kind, p, name)
                        t = lagged(kind, p, i)
                        if t is not None:
                            turn(n, p, t, i < LAG)

            all_pairs(pe, pair)

            total = number(PAIRS - 1, LAST, 1, "pv0")
            pe.wait_ge(o_w_hi, PAIRS)
            pe.wait_ge(o_w_lo, PAIRS)
            pe.wait_ge(unit_used, total)
            project_out(total % 2, 0)
            turn(PAIRS, 0, NT - 2, True)
            free_bank(total + 2)
            project_out((total + 1) % 2, 1)
            turn(PAIRS, 0, NT - 1, True)
            pe.wait_ge(p_lo, groups_to(PAIRS, 0, -1))
            free_bank(total + 3)
            context((total + 2) % 2, 1, 1)
            pe.wait_ge(unit_used, total + 3)
            project_out((total + 3) % 2, 2)
            free_bank(total + 5)
            project_out((total + 4) % 2, 3)

            for u in range(2 * FT):
                f, c = u % FT, u // FT
                if c == 0:
                    pe.wait_ge(ffn_w_lo, f + 1)
                if u >= 2:
                    pe.wait_ge(h_ready, u - 1)
                else:
                    pe.wait_ge(scores_masked, HEADS * NT)
                for which in range(2):
                    for kk in range(KT):
                        at = f * PIECE + (which * KT + kk) * P
                        last = three(ps_s[:, u % 2, which * HALF:(which + 1) * HALF],
                                     [ffn_w(0, at), ffn_w(1, at)],
                                     both(xn_t, slice(None), kk, slice(c * HALF, c * HALF + HALF)),
                                     kk == 0, kk == KT - 1)
                last.then_inc(gate_up_done, 1)
            pe.wait_ge(ffn_w_lo, PIECES)
            pe.wait_ge(p_lo, HEADS * HEAD_GROUPS)
            for d in range(NT // 2):
                if d >= 2:
                    pe.wait_ge(out_ready, d - 1)
                c = d // 2
                pe.wait_ge(h_lo_done, (c + 1) * FT)
                for t in range(2):
                    q = ((2 * d + t) % 4) * P
                    for f in range(FT):
                        u, at = c * FT + f, FT * PIECE + f * HID
                        last = three(ps_t[:, d % 2, t * HID:(t + 1) * HID],
                                     [h_tile(0, u)[:, q:q + P], h_tile(1, u)[:, q:q + P]],
                                     [ffn_w(0, at, HID), ffn_w(1, at, HID)], f == 0, f == FT - 1)
                last.then_inc(down_done, 1)

        @block.scalar
        def _(act):
            act.wait_ge(ln_step, 2)
            act.activation(ln[:, 1, :], ln[:, 0, :], ACT.Sqrt).then_inc(root_done, 1)

            act.wait_ge(qk_landed, 16)
            act.activation(qk_w[0][:, 0, :, :], qk_raw[:, :, :], ACT.Copy).then_inc(qk_w_hi, 1)
            for part in range(4):
                c, kk = part // 2, part % 2
                act.wait_ge(xn_turned, part + 1)
                act.activation(xn_t[0][:, kk, c * HALF:(c + 1) * HALF],
                               ps_s[:, kk, c * HALF:(c + 1) * HALF], ACT.Copy).then_inc(xn_hi, 1)
            def hi_of(n, p, name, bank, no):
                act.wait_ge(unit_done, no)
                b = unit_bias(p, name)
                if b is None:
                    act.activation(unit_place(0, p, name), ps_u[:, bank, :], ACT.Copy).then_inc(unit_hi, 1)
                else:
                    act.activation(unit_place(0, p, name), ps_u[:, bank, :], ACT.Identity,
                                   bias=b).then_inc(unit_hi, 1)

            act.wait_ge(bias_ready, 1)
            hi_of(0, 0, "q0", 0, 1)
            hi_of(0, 0, "k0", 1, 2)
            act.wait_ge(v_landed, 16)
            act.activation(v_w[0][:, :, :], v_raw[:, :, :], ACT.Copy).then_inc(v_w_hi, 1)
            act.wait_ge(qk_landed, 32)
            act.activation(qk_w[0][:, 1, :, :], qk_raw[:, :, :], ACT.Copy).then_inc(qk_w_hi, 1)

            def exp(n, p, i):
                act.wait_ge(scores_masked, tile_no(n, p, i) + 1)
                col = p * NT + i
                act.activation(slot(i), slot(i), ACT.Exp, bias=neg_max[:, col:col + 1], scale=-1.0,
                               accum_out=row_sum[:, col:col + 1]).then_inc(exp_done, 1)

            def p_hi_of(n, p, i, back):
                for g in range(GROUPS[i]):
                    room = (GROUPS_BEFORE[i] + g) % 2
                    act.wait_ge(p_turned, groups_to(n, p, i - NT - 1 if back else i - 1) + g + 1)
                    act.activation(p_rows(0, i, g),
                                   ps_t[:, room, 0:len(turned(i, g)) * P].rearrange("p (j q) -> p j q", q=P),
                                   ACT.Copy).then_inc(p_hi, 1)

            act.wait_ge(cleared, 2)

            def pair(n, kind):
                for p in range(2):
                    for i in range(NT):
                        if i == 2 and not (kind == LAST and p == 1):
                            act.wait_ge(bias_ready, 4 * n + 2 * p + 2)
                        if i == 6:
                            act.wait_ge(bias_ready, 4 * n + 2 * p + 1)
                        todo = [name for name, step in units_of(kind, p) if step == i and is_split(name)]
                        if todo and "pv" not in todo[0]:
                            name = todo.pop(0)
                            hi_of(n, p, name, bank_of(kind, p, name), number(n, kind, p, name))
                        exp(n, p, i)
                        for name in todo:
                            hi_of(n, p, name, bank_of(kind, p, name), number(n, kind, p, name))
                        t = lagged(kind, p, i)
                        if t is not None:
                            p_hi_of(n, p, t, i < LAG)
                        if i == 4 and kind != LAST:
                            act.wait_ge(qk_landed, n * 32 + (p + 3) * 16)
                            act.wait_ge(unit_done, number(n, kind, p, "k1"))
                            act.activation(qk_w[0][:, p, :, :], qk_raw[:, :, :], ACT.Copy).then_inc(qk_w_hi, 1)
                        if i == 5 and p == 1 and kind != LAST:
                            act.wait_ge(v_landed, n * 16 + 32)
                            act.wait_ge(unit_done, number(n, kind, 0, "v3"))
                            act.activation(v_w[0][:, :, :], v_raw[:, :, :], ACT.Copy).then_inc(v_w_hi, 1)
                        if i == 2 and p == 1:
                            act.wait_ge(o_landed, n * 16 + 16)
                            if kind != FIRST:
                                act.wait_ge(unit_done, number(n, kind, 0, "_out3"))
                            act.activation(o_w[0][:, :, :], o_raw[:, :, :], ACT.Copy).then_inc(o_w_hi, 1)

            all_pairs(act, pair)

            total = number(PAIRS - 1, LAST, 1, "pv0")
            p_hi_of(PAIRS, 0, NT - 2, True)
            p_hi_of(PAIRS, 0, NT - 1, True)
            hi_of(PAIRS, 0, "_pv1", (total + 2) % 2, total + 3)

            def ffn_w_hi_of(piece):
                at = piece * PIECE
                act.activation(ffn_w(0, at, PIECE), w_ffn[:, at:at + PIECE], ACT.Copy).then_inc(ffn_w_hi, 1)

            act.wait_ge(term_added, LUT * NT)
            for piece in range(3):
                ffn_w_hi_of(piece)
            for u in range(2 * FT):
                act.wait_ge(gate_up_done, u + 1)
                if u >= 2:
                    act.wait_ge(h_ready, u - 1)
                act.activation(work[:, (u % 2) * HALF:(u % 2 + 1) * HALF], ps_s[:, u % 2, 0:HALF],
                               ACT.Silu).then_inc(silu_done, 1)
                if u + 3 < PIECES:
                    ffn_w_hi_of(u + 3)
                act.wait_ge(h_ready, u + 1)
                act.activation(h_tile(0, u), work[:, (2 + u % 2) * HALF:(3 + u % 2) * HALF],
                               ACT.Copy).then_inc(h_hi_done, 1)

        @block.vector
        def _(dve):
            for t in range(NT):
                if t % 4 == 0:
                    dve.wait_ge(x_landed[t // 4], 16)
                last = dve.bn_stats(stats[:, t, :], acc[:, t, :])
            last.then_inc(ln_step, 1)
            dve.wait_ge(ln_step, 1)
            for t in range(NT):
                last = dve.bn_aggr(moments[:, t, :], stats[:, t, :])
            last.then_inc(cleared, 1)
            dve.wait_ge(cleared, 1)
            dve.tensor_scalar(ln[:, 0, :], moments[:, :, 1], EPS, None, ALU.add).then_inc(ln_step, 1)
            dve.wait_ge(root_done, 1)
            dve.reciprocal(ln[:, 2, :], ln[:, 1, :]).then_inc(ln_step, 1)
            dve.wait_ge(ln_step, 3)
            dve.tensor_tensor(ln[:, 3, :], ln[:, 2, :], ln[:, 2, :], ALU.mult).then_inc(ln_step, 1)
            dve.wait_ge(ln_step, 4)
            dve.tensor_tensor(ln[:, 3, :], ln[:, 3, :], ln[:, 0, :], ALU.mult).then_inc(ln_step, 1)
            dve.wait_ge(ln_step, 5)
            dve.tensor_scalar(ln[:, 3, :], ln[:, 3, :], -0.5, 1.5, ALU.mult, ALU.add).then_inc(ln_step, 1)
            dve.wait_ge(ln_step, 6)
            dve.tensor_tensor(ln[:, 2, :], ln[:, 2, :], ln[:, 3, :], ALU.mult).then_inc(ln_step, 1)
            dve.wait_ge(ln_step, 7)
            for t in range(NT):
                dve.tensor_scalar(xn[:, t, :], acc[:, t, :], moments[:, t, 0:1], ln[:, 2, t:t + 1],
                                  ALU.subtract, ALU.mult).then_inc(xn_ready, 1)
            zero0, zero1 = pt_at(0, 3) + 2 * P, pt_at(1, 7) + 2 * P
            for part in range(2):
                dve.memset(p_t[part][:, zero0:zero0 + P].bitcast(F32), 0.0)
                last = dve.memset(p_t[part][:, zero1:zero1 + P].bitcast(F32), 0.0)
            last.then_inc(cleared, 1)
            for part in range(4):
                c, kk = part // 2, part % 2
                dve.wait_ge(xn_hi, part + 1)
                at = slice(c * HALF, (c + 1) * HALF)
                dve.tensor_tensor(xn_t[1][:, kk, at], ps_s[:, kk, at], xn_t[0][:, kk, at].bitcast(F32),
                                  ALU.subtract).then_inc(xn_lo, 1)

            def lo_of(n, p, name, bank, no):
                dve.wait_ge(unit_hi, no)
                b, hi = unit_bias(p, name), unit_place(0, p, name).bitcast(F32)
                if b is None:
                    dve.tensor_tensor(unit_place(1, p, name), ps_u[:, bank, :], hi,
                                      ALU.subtract).then_inc(unit_used, 1)
                else:
                    dve.scalar_tensor_tensor(unit_place(1, p, name), ps_u[:, bank, :], b, hi,
                                             ALU.add, ALU.subtract).then_inc(unit_used, 1)

            def next_bias(n, p, parity, which):
                at = slice(2 * n + p, 2 * n + p + 1) if isinstance(n, int) else bass.ds(2 * n + p, 1)
                dve.tensor_copy(bias_now[:, parity, which],
                                bias[:, at, which].rearrange("p a b -> p (a b)")).then_inc(bias_ready, 1)

            def make_alibi(n, p, parity):
                dve.tensor_scalar(alibi[:, parity, :], distance[:, :], column(slope, n, p), None,
                                  ALU.mult).then_inc(alibi_ready, 1)

            dve.wait_ge(made, 3 + LUT)
            make_alibi(0, 0, 0)
            dve.wait_ge(bias_landed, 16)
            next_bias(0, 0, 0, slice(0, 3))
            dve.wait_ge(bias_ready, 1)
            lo_of(0, 0, "q0", 0, 1)
            lo_of(0, 0, "k0", 1, 2)
            dve.wait_ge(small_landed, 32)
            for t in range(NT):
                last = dve.tensor_tensor(acc[:, t, :], acc[:, t, :], term[:, 0, 0:HID], ALU.add)
            last.then_inc(cleared, 1)
            dve.wait_ge(idx_landed, 16)
            dve.tensor_copy(codes[:, :], w_ffn[:, :].bitcast(I32)).then_inc(codes_ready, 1)
            dve.wait_ge(codes_ready, 1)
            dve.memset(w_ffn[:, :], 0.0).then_inc(cleared, 1)
            dve.wait_ge(cleared, 4)

            def mask(n, kind, p, i):
                dve.wait_ge(scores_done, tile_no(n, p, i) + 1)
                if i == 0:
                    dve.wait_ge(alibi_ready, 2 * n + p + 1)
                if not (kind == FIRST and p == 0 and i < 4):
                    dve.wait_ge(p_turned, groups_to(n, p, i - 4))
                width, col = (i + 1) * P, p * NT + i
                dve.memset(pad[:, col:col + 1], 0.0)
                dve.tensor_tensor_reduce(slot(i), ps_s[:, i % 2, 0:width], alibi[:, p, S - width:S],
                                         -1.0, 3.0e38, ALU.add, ALU.min,
                                         neg_max[:, col:col + 1]).then_inc(scores_masked, 1)

            def p_lo_of(n, p, i, back):
                for g in range(GROUPS[i]):
                    room = (GROUPS_BEFORE[i] + g) % 2
                    dve.wait_ge(p_hi, groups_to(n, p, i - NT - 1 if back else i - 1) + g + 1)
                    dve.tensor_tensor(p_rows(1, i, g),
                                      ps_t[:, room, 0:len(turned(i, g)) * P].rearrange("p (j q) -> p j q", q=P),
                                      p_rows(0, i, g).bitcast(F32), ALU.subtract).then_inc(p_lo, 1)

            def add_out(c, bank, no):
                dve.wait_ge(unit_done, no)
                dve.wait_ge(unit_used, no - 1)
                rows = acc[:, 2 * c:2 * c + 2, :].rearrange("p t h -> p (t h)")
                dve.tensor_tensor(rows, ps_u[:, bank, :], rows, ALU.add).then_inc(unit_used, 1)

            def pair(n, kind):
                for p in range(2):
                    for i in range(NT):
                        mask(n, kind, p, i)
                        if i == 1 and not (kind == LAST and p == 1):
                            next_bias(n, p + 1, 1 - p, slice(0, 2))
                        if i == 2 and not (kind == LAST and p == 1):
                            dve.wait_ge(bias_ready, 4 * n + 2 * p + 2)
                        if i == 5 and not (kind == LAST and p == 1):
                            next_bias(n, p + 1, 1 - p, slice(2, 3))
                        if i == 6:
                            dve.wait_ge(bias_ready, 4 * n + 2 * p + 1)
                        for name, step in units_of(kind, p):
                            if step != i:
                                continue
                            if is_split(name):
                                lo_of(n, p, name, bank_of(kind, p, name), number(n, kind, p, name, is_split))
                            else:
                                add_out(int(name[-1]), bank_of(kind, p, name), number(n, kind, p, name))
                        dve.wait_ge(exp_done, tile_no(n, p, i) + 1)
                        col = p * NT + i
                        dve.reciprocal(inv_sum[:, col:col + 1], row_sum[:, col:col + 1]).then_inc(inv_ready, 1)
                        t = lagged(kind, p, i)
                        if t is not None:
                            p_lo_of(n, p, t, i < LAG)
                        piece = slice(i * LUT_PIECE, (i + 1) * LUT_PIECE)
                        if not (kind == FIRST and p == 0 and i < 2):
                            dve.wait_ge(term_added, tile_no(n, p, i) - 1)
                        dve.tensor_scalar(term[:, i % 2, :], codes[:, piece], column(entry, n, p),
                                          column(table, n, p), ALU.is_equal, ALU.mult).then_inc(term_ready, 1)
                        if i == 5 and not (kind == LAST and p == 1):
                            make_alibi(n, p + 1, 1 - p)

            all_pairs(dve, pair)

            total = number(PAIRS - 1, LAST, 1, "pv0")
            splits = number(PAIRS - 1, LAST, 1, "pv0", is_split)
            add_out(0, total % 2, total + 1)
            p_lo_of(PAIRS, 0, NT - 2, True)
            add_out(1, (total + 1) % 2, total + 2)
            p_lo_of(PAIRS, 0, NT - 1, True)
            lo_of(PAIRS, 0, "_pv1", (total + 2) % 2, splits + 1)
            add_out(2, (total + 3) % 2, total + 4)
            add_out(3, (total + 4) % 2, total + 5)

            for u in range(2 * FT):
                dve.wait_ge(silu_done, u + 1)
                if u >= 2:
                    dve.wait_ge(h_lo_done, u - 1)
                h = work[:, (2 + u % 2) * HALF:(3 + u % 2) * HALF]
                dve.tensor_tensor(h, ps_s[:, u % 2, HALF:2 * HALF], work[:, (u % 2) * HALF:(u % 2 + 1) * HALF],
                                  ALU.mult).then_inc(h_ready, 1)
                dve.wait_ge(h_hi_done, u + 1)
                dve.tensor_tensor(h_tile(1, u), h, h_tile(0, u).bitcast(F32), ALU.subtract).then_inc(h_lo_done, 1)
            for d in range(NT // 2):
                dve.wait_ge(down_done, d + 1)
                dve.wait_ge(unit_used, total + 5)
                rows = acc[:, 2 * d:2 * d + 2, :].rearrange("p t h -> p (t h)")
                dve.tensor_tensor(rows, ps_t[:, d % 2, :], rows, ALU.add).then_inc(out_ready, 1)

        @block.gpsimd
        def _(pool):
            pool.memset(ident[:, :], 0.0).then_inc(made, 1)
            pool.wait_ge(made, 1)
            pool.affine_select(out=ident[:, :], in_=ident[:, :], compare_op=ALU.not_equal, fill=1.0, base=0,
                               pattern=[[-1, P]], channel_multiplier=1).then_inc(made, 1)
            pool.iota(distance[:, :], pattern=[[1, S]], base=-(S - P), channel_multiplier=-1,
                      allow_small_or_imprecise_dtypes=True).then_inc(iota_done, 1)
            pool.wait_ge(iota_done, 1)
            pool.affine_select(out=distance[:, :], in_=distance[:, :], compare_op=ALU.is_ge, fill=MASKED,
                               base=S - P, pattern=[[-1, S]], channel_multiplier=1).then_inc(made, 1)
            for h in range(HEADS):
                pool.memset(slope[:, h:h + 1], 1.0 / 2.0 ** (h / 2.0)).then_inc(made, 1)
            pool.iota(entry[:, :], pattern=[[1, LUT]], base=0, channel_multiplier=0,
                      allow_small_or_imprecise_dtypes=True).then_inc(made, 1)

            def qk_lo(no, parity):
                pool.wait_ge(qk_w_hi, no)
                pool.tensor_tensor(qk_w[1][:, parity, :, :], qk_raw[:, :, :], qk_w[0][:, parity, :, :].bitcast(F32),
                                   ALU.subtract).then_inc(qk_w_lo, 1)

            def v_lo(no):
                pool.wait_ge(v_w_hi, no)
                pool.tensor_tensor(v_w[1][:, :, :], v_raw[:, :, :], v_w[0][:, :, :].bitcast(F32),
                                   ALU.subtract).then_inc(v_w_lo, 1)

            qk_lo(1, 0)
            v_lo(1)
            qk_lo(2, 1)
            pool.wait_ge(cleared, 4)

            def pair(n, kind):
                for p in range(2):
                    for i in range(NT):
                        col = p * NT + i
                        pool.wait_ge(inv_ready, tile_no(n, p, i) + 1)
                        pool.tensor_tensor(pad[:, 2 * NT + col:2 * NT + col + 1], entry[:, 0:1], entry[:, 0:1], ALU.add)
                        pool.tensor_scalar(slot(i), slot(i), inv_sum[:, col:col + 1], 1.0, ALU.mult,
                                           ALU.mult).then_inc(normed, 1)
                        if i == 4 and kind != LAST:
                            qk_lo(2 * n + p + 3, p)
                        if i == 5 and p == 1 and kind != LAST:
                            v_lo(n + 2)
                        if i == 2 and p == 1:
                            pool.wait_ge(o_w_hi, n + 1)
                            pool.tensor_tensor(o_w[1][:, :, :], o_raw[:, :, :], o_w[0][:, :, :].bitcast(F32),
                                               ALU.subtract).then_inc(o_w_lo, 1)
                        pool.wait_ge(term_ready, tile_no(n, p, i) + 1)
                        if not (kind == FIRST and p == 0):
                            pool.wait_ge(term_added, tile_no(n, p, i) - NT + 1)
                        piece = w_ffn[:, i * LUT_PIECE:(i + 1) * LUT_PIECE]
                        pool.tensor_tensor(piece, piece, term[:, i % 2, :], ALU.add).then_inc(term_added, 1)

            all_pairs(pool, pair)

            for piece in range(PIECES):
                at = piece * PIECE
                pool.wait_ge(ffn_w_hi, piece + 1)
                pool.tensor_tensor(ffn_w(1, at, PIECE), w_ffn[:, at:at + PIECE],
                                   ffn_w(0, at, PIECE).bitcast(F32), ALU.subtract).then_inc(ffn_w_lo, 1)


def kernel(**inputs):
    import numpy as np
    import concourse.bacc as bacc
    from concourse.bass_utils import run_bass_kernel_spmd

    def heads(w, per):
        return w.reshape(KT, P, HEADS // per, per * D).transpose(2, 1, 0, 3)

    w = np.asarray(inputs["L0_attn_qkv_w"]).reshape(HID, 3, HEADS * D)
    w_qk = np.concatenate([heads(w[:, 0], 1), heads(w[:, 1], 1)], axis=3)
    w_v = heads(w[:, 2], 2)
    w_o = np.asarray(inputs["L0_attn_out_w"]).reshape(PAIRS, 2, D, HID).transpose(0, 2, 1, 3)
    b_qkv = np.asarray(inputs["L0_attn_qkv_b"]).reshape(3, HEADS, D).transpose(2, 1, 0)

    pad = ((0, FT * P - INTER), (0, 0))
    gate, up = (np.pad(np.asarray(inputs[f"L0_ffn_{s}_idx"]), pad, constant_values=LUT)
                .reshape(FT, P, KT, P).transpose(3, 0, 2, 1) for s in ("gate", "up"))
    down = np.pad(np.asarray(inputs["L0_ffn_down_idx"]).T, pad, constant_values=LUT)
    idx = np.concatenate([np.stack([gate, up], axis=2).reshape(P, FT * PIECE),
                          down.reshape(FT, P, HID).transpose(1, 0, 2).reshape(P, FT * HID)], axis=1)
    arrays = {
        "x": np.asarray(inputs["L0_attn_x"]).reshape(S, HID), "w_qk": w_qk, "w_v": w_v, "w_o": w_o,
        "b_qkv": b_qkv, "b_out": np.asarray(inputs["L0_attn_out_b"]),
        "lut": np.asarray(inputs["L0_ffn_lut"]), "idx": idx,
    }
    arrays = {name: np.ascontiguousarray(a) for name, a in arrays.items()}
    nc = bacc.Bacc("TRN2", target_bir_lowering=False, num_devices=1)
    args = [nc.dram_tensor(name, a.shape, mybir.dt.from_np(a.dtype), kind="ExternalInput").ap()
            for name, a in arrays.items()]
    out = nc.dram_tensor("out", (S, HID), F32, kind="ExternalOutput").ap()
    block_ffn(nc, *args, out)
    r = run_bass_kernel_spmd(nc, [arrays], core_ids=[0])
    return r.results[0]["out"].reshape(1, S, HID)
```

```python
from contextlib import ExitStack

import concourse.bass as bass
from concourse import mybir

ALU = mybir.AluOpType
ACT = mybir.ActivationFunctionType
F32 = mybir.dt.float32
F32R = mybir.dt.float32r
I32 = mybir.dt.int32
U8 = mybir.dt.uint8

P = 128
S, HID, HEADS, D = 1024, 256, 16, 128
INTER, LUT = 688, 16
EPS = 1e-5
KT = HID // P
NT = S // P
HALF = 512
PAIRS = HEADS // 2
FT = -(-INTER // P)
MASKED = -1.0e38
LAG = 3

GROUPS = [-(-(i + 1) // 4) for i in range(NT)]
GROUPS_BEFORE = [sum(GROUPS[:i]) for i in range(NT + 1)]
HEAD_GROUPS = GROUPS_BEFORE[NT]

SLOT_W = [(i + 5) * P for i in range(4)]
SLOT_AT = [sum(SLOT_W[:i]) for i in range(4)]

PT_TIGHT, PT_ROW = 384, HALF
PT_HALF0 = 3 * PT_TIGHT + HALF
PT_WIDE = 2 * PT_HALF0
PT_COLS = PT_WIDE + 4 * PT_ROW

PIECE = 4 * P
PIECES = FT + FT * HID // PIECE
WF = PIECES * PIECE
TERMS = 4
LUT_PIECE = WF // TERMS


def pt_at(half, j):
    if half == 0:
        return PT_HALF0 + j * PT_TIGHT
    return PT_WIDE + j * PT_ROW if j < 4 else (j - 4) * PT_TIGHT


def pt_from(half, j):
    return min(max(0, j - 4 * half) * P, 2 * P)


UNITS = [
    (("q1", 0), ("k1", 1), ("_out0", 2), ("nq0", 2), ("_out1", 3), ("_pv1-", 3), ("_pv1", 4),
     ("v0", 5), ("nk0", 5), ("v1", 6), ("v2", 6), ("pv0", 7)),
    (("_out2", 0), ("q1", 0), ("k1", 1), ("v3", 1), ("_out3", 2), ("_pv1-", 3), ("_pv1", 4), ("nq0", 5),
     ("nk0", 6), ("pv0", 7)),
]
TAIL = (("turn", 5), ("gate_up", 0), ("turn", 6), ("out", 0), ("gate_up", 1), ("turn", 7), ("out", 1),
        ("gate_up", 2), ("pv", 1), ("gate_up", 3), ("out", 2), ("out", 3)) + tuple(
            ("gate_up", u) for u in range(4, 2 * FT))
FIRST, STEADY, LAST = "first", "steady", "last"


def units_of(kind, p, begun=False):
    return [(name, step) for name, step in UNITS[p] if (begun or name[-1] != "-")
            and not (kind == FIRST and (name[:4] == "_out" or p == 0 and name[0] == "_"))
            and not (kind == LAST and p == 1 and name[0] == "n")]


def is_split(name):
    return "out" not in name


def counted(kind, only):
    return [(p, name) for p in range(2) for name, _ in units_of(kind, p) if only(name)]


def number(n, kind, p, name, only=lambda name: True):
    here = counted(kind, only).index((p, name)) + 1
    per = len(counted(STEADY, only))
    return n * per + 2 + here - (0 if kind == FIRST else per - len(counted(FIRST, only)))


def bank_of(kind, p, name):
    return (number(0 if kind == FIRST else 2, kind, p, name) - 1) % 2


def block_ffn(nc, x, w_qk, w_v, w_o, b_qkv, b_out, lut, idx, out):
    with ExitStack() as ctx:
        def sb(name, shape, dt=F32):
            return ctx.enter_context(nc.sbuf_tensor(name, shape, dt))

        def sem(name):
            return ctx.enter_context(nc.semaphore(name))

        acc = sb("acc", [P, NT, HID])
        work = sb("work", [P, sum(SLOT_W)])
        xn_t = [sb(f"xn_t_{s}", [P, KT, S], F32R) for s in ("hi", "lo")]
        qk = [sb(f"qk_{s}", [P, 2, 2, S], F32R) for s in ("hi", "lo")]
        v = [sb(f"v_{s}", [P, NT, 2 * D], F32R) for s in ("hi", "lo")]
        p_t = [sb(f"p_t_{s}", [P, PT_COLS], F32R) for s in ("hi", "lo")]
        ctx_t = [sb(f"ctx_t_{s}", [P, 2, S], F32R) for s in ("hi", "lo")]
        qk_raw = sb("qk_raw", [P, KT, 2 * D])
        qk_w = [sb(f"qk_w_{s}", [P, 2, KT, 2 * D], F32R) for s in ("hi", "lo")]
        v_raw = sb("v_raw", [P, KT, 2 * D])
        v_w = [sb(f"v_w_{s}", [P, KT, 2 * D], F32R) for s in ("hi", "lo")]
        o_raw = sb("o_raw", [P, 2, HID])
        o_w = [sb(f"o_w_{s}", [P, 2, HID], F32R) for s in ("hi", "lo")]
        distance = sb("distance", [P, S])
        alibi = sb("alibi", [P, 2, S])
        codes = sb("codes", [P, WF], U8)
        w_ffn = sb("w_ffn", [P, WF])
        term = sb("term", [P, LUT_PIECE])
        ident = sb("ident", [P, P])
        bias = sb("bias", [P, HEADS, 3])
        bias_now = sb("bias_now", [P, 2, 3])
        table = sb("table", [P, LUT])
        entry = sb("entry", [P, LUT])
        slope = sb("slope", [P, HEADS])
        pad = sb("pad", [P, 4 * NT])
        neg_max = sb("neg_max", [P, 2 * NT])
        row_sum = sb("row_sum", [P, 2 * NT])
        inv_sum = sb("inv_sum", [P, 2 * NT])
        stats = sb("stats", [P, NT, 6])
        moments = sb("moments", [P, NT, 2])
        ln = sb("ln", [P, 4, NT])

        ps_s = ctx.enter_context(nc.psum_tensor("ps_s", [P, 2, S], F32))
        ps_t = ctx.enter_context(nc.psum_tensor("ps_t", [P, 2, HALF], F32))
        ps_u = ctx.enter_context(nc.psum_tensor("ps_u", [P, 2, HALF], F32))

        x_landed, bias_landed, small_landed = [sem("x0_landed"), sem("x1_landed")], sem("bias_landed"), sem("small_landed")
        idx_landed, qk_landed = sem("idx_landed"), sem("qk_landed")
        v_landed, o_landed, stored = sem("v_landed"), sem("o_landed"), sem("stored")
        xn_turned, scores_done, p_turned = sem("xn_turned"), sem("scores_done"), sem("p_turned")
        unit_done, gate_up_done, down_done = sem("unit_done"), sem("gate_up_done"), sem("down_done")
        root_done, xn_hi, exp_done, p_hi = sem("root_done"), sem("xn_hi"), sem("exp_done"), sem("p_hi")
        unit_hi, qk_w_hi, v_w_hi, o_w_hi = sem("unit_hi"), sem("qk_w_hi"), sem("v_w_hi"), sem("o_w_hi")
        ffn_w_hi, silu_done, h_hi_done = sem("ffn_w_hi"), sem("silu_done"), sem("h_hi_done")
        ln_step, xn_ready, xn_lo = sem("ln_step"), sem("xn_ready"), sem("xn_lo")
        bias_ready = sem("bias_ready")
        cleared, codes_ready, alibi_ready = sem("cleared"), sem("codes_ready"), sem("alibi_ready")
        scores_masked, inv_ready, p_lo = sem("scores_masked"), sem("inv_ready"), sem("p_lo")
        unit_used, term_ready = sem("unit_used"), sem("term_ready")
        h_ready, h_lo_done, out_ready = sem("h_ready"), sem("h_lo_done"), sem("out_ready")
        based = sem("based")
        iota_done, made, normed, term_added = sem("iota_done"), sem("made"), sem("normed"), sem("term_added")
        qk_w_lo, v_w_lo, o_w_lo, ffn_w_lo = sem("qk_w_lo"), sem("v_w_lo"), sem("o_w_lo"), sem("ffn_w_lo")

        block = ctx.enter_context(nc.Block())

        xn = work[:, 0:NT * HID].rearrange("p (t h) -> p t h", t=NT)

        def slot(i, width=None):
            at = SLOT_AT[i % 4]
            return work[:, at:at + (width or (i + 1) * P)]

        def turned(i, g):
            return range(4 * g, min(4 * g + 4, i + 1))

        def p_rows(part, i, g):
            half, js = i // 4, turned(i, g)
            at, step = pt_at(half, js[0]), (PT_ROW if half and g == 0 else PT_TIGHT)
            q = (i % 4) * P
            if step == PT_ROW:
                rows = p_t[part][:, at:at + 4 * step].rearrange("p (j q) -> p j q", q=step)
                return rows[:, 0:len(js), q:q + P]
            rows = p_t[part][:, at + q:at + q + len(js) * step].rearrange("p (j q) -> p j q", q=step)
            return rows[:, :, 0:P]

        def tile_no(n, p, i):
            return n * (2 * NT) + p * NT + i

        def groups_to(n, p, i):
            if i < 0:
                return n * (2 * HEAD_GROUPS) + (p - 1) * HEAD_GROUPS + GROUPS_BEFORE[i + NT + 1]
            return n * (2 * HEAD_GROUPS) + p * HEAD_GROUPS + GROUPS_BEFORE[i + 1]

        def lagged(kind, p, i):
            if i >= LAG:
                return i - LAG
            return None if kind == FIRST and p == 0 else i - LAG + NT

        def parity_of(p, name):
            return 1 - p if name[0] in "n_" else p

        def unit_place(part, p, name):
            pr, c = parity_of(p, name), int(name[-1])
            if "q" in name or "k" in name:
                return qk[part][:, pr, int("k" in name), c * HALF:(c + 1) * HALF]
            if "pv" in name:
                return ctx_t[part][:, pr, c * HALF:(c + 1) * HALF]
            return v[part][:, 2 * c:2 * c + 2, :].rearrange("p t d -> p (t d)")

        def unit_bias(p, name):
            if "pv" not in name and "v" in name:
                return None
            which = 2 if "pv" in name else int("k" in name)
            return bias_now[:, parity_of(p, name), which:which + 1]

        def column(tensor, n, p):
            if isinstance(n, int):
                return tensor[:, 2 * n + p:2 * n + p + 1]
            return tensor[:, bass.ds(2 * n + p, 1)]

        def ffn_w(part, piece, at=0, width=PIECE):
            if piece < 4:
                at += (piece % 2) * PIECE
                return qk[part][:, 0, piece // 2, at:at + width]
            at += (piece - 4) * PIECE
            return p_t[part][:, at:at + width]

        def h_tile(part, u):
            at = (u % 4) * HALF
            room = (qk[part][:, 1, :, :], v[part][:, :, :], ctx_t[part][:, :, :])[u // 4]
            return room.rearrange("p a b -> p (a b)")[:, at:at + HALF]

        def silu_tile(u):
            return term[:, (u % 2) * HALF:(u % 2 + 1) * HALF]

        def h_raw(u):
            return alibi[:, 0, (u % 2) * HALF:(u % 2 + 1) * HALF]

        def all_pairs(engine, pair):
            pair(0, FIRST)
            with engine.Fori(1, PAIRS - 1) as n:
                pair(n, STEADY)
            pair(PAIRS - 1, LAST)

        @block.sync
        def _(sp):
            x_t = x.rearrange("(t p) h -> p t h", p=P)
            for c in range(2):
                sp.dma_start(acc[:, 4 * c:4 * c + 4, :], x_t[:, 4 * c:4 * c + 4, :]).then_inc(x_landed[c], 16)
            sp.dma_start(qk_raw[:, :, :], w_qk[0]).then_inc(qk_landed, 16)
            sp.dma_start(bias[:, :, :], b_qkv).then_inc(bias_landed, 16)
            sp.dma_start(v_raw[:, :, :], w_v[0]).then_inc(v_landed, 16)
            sp.dma_start(table[:, :], lut.partition_broadcast(P)).then_inc(small_landed, 16)
            sp.dma_start(term[:, 0:HID], b_out.partition_broadcast(P)).then_inc(small_landed, 16)
            sp.dma_start(w_ffn[:, :].bitcast(I32), idx).then_inc(idx_landed, 16)
            sp.dma_start(o_raw[:, :, :], w_o[0]).then_inc(o_landed, 16)
            for h in (1, 2):
                sp.wait_ge(qk_w_hi, h)
                sp.wait_ge(qk_w_lo, h)
                sp.dma_start(qk_raw[:, :, :], w_qk[h]).then_inc(qk_landed, 16)
            sp.wait_ge(v_w_hi, 1)
            sp.wait_ge(v_w_lo, 1)
            sp.dma_start(v_raw[:, :, :], w_v[1]).then_inc(v_landed, 16)

            def refill(n, to_the_end):
                sp.wait_ge(qk_w_hi, n * 2 + 3)
                sp.wait_ge(qk_w_lo, n * 2 + 3)
                sp.dma_start(qk_raw[:, :, :], w_qk[n * 2 + 3]).then_inc(qk_landed, 16)
                if not to_the_end:
                    sp.wait_ge(v_w_hi, n + 2)
                    sp.wait_ge(v_w_lo, n + 2)
                    sp.dma_start(v_raw[:, :, :], w_v[n + 2]).then_inc(v_landed, 16)
                    sp.wait_ge(qk_w_hi, n * 2 + 4)
                    sp.wait_ge(qk_w_lo, n * 2 + 4)
                    sp.dma_start(qk_raw[:, :, :], w_qk[n * 2 + 4]).then_inc(qk_landed, 16)
                sp.wait_ge(o_w_hi, n + 1)
                sp.wait_ge(o_w_lo, n + 1)
                sp.dma_start(o_raw[:, :, :], w_o[n + 1]).then_inc(o_landed, 16)

            with sp.Fori(0, PAIRS - 2) as n:
                refill(n, False)
            refill(PAIRS - 2, True)
            out_t = out.rearrange("(t p) h -> p t h", p=P)
            for d in range(NT // 2):
                sp.wait_ge(out_ready, d + 1)
                sp.dma_start(out_t[:, 2 * d:2 * d + 2, :], acc[:, 2 * d:2 * d + 2, :]).then_inc(stored, 16)
            sp.wait_ge(stored, 16 * (NT // 2))

        @block.tensor
        def _(pe):
            def three(out, lhs, rhs, first, last):
                pe.matmul(out, lhs[0], rhs[0], start=first, stop=False)
                pe.matmul(out, lhs[0], rhs[1], start=False, stop=False)
                return pe.matmul(out, lhs[1], rhs[0], start=False, stop=last)

            def both(tensor, *where):
                return [t[where] for t in tensor]

            def free_bank(no):
                if isinstance(no, int) and no <= 2:
                    return
                pe.wait_ge(unit_used, no - 2)

            def project(bank, which, pr, c):
                for kk in range(KT):
                    last = three(ps_u[:, bank, :],
                                 both(qk_w, slice(None), pr, kk, slice(which * D, which * D + D)),
                                 both(xn_t, slice(None), kk, slice(c * HALF, c * HALF + HALF)),
                                 kk == 0, kk == KT - 1)
                last.then_inc(unit_done, 1)

            def values(bank, c):
                for t in (2 * c, 2 * c + 1):
                    for kk in range(KT):
                        last = three(ps_u[:, bank, (t % 2) * 2 * D:(t % 2 + 1) * 2 * D],
                                     both(xn_t, slice(None), kk, slice(t * P, t * P + P)),
                                     both(v_w, slice(None), kk, slice(None)),
                                     kk == 0, kk == KT - 1)
                last.then_inc(unit_done, 1)

            def context(bank, pr, c, js):
                tiles = 4 * c + 4
                for j in js:
                    q, at = pt_from(c, j), pt_at(c, j)
                    last = three(ps_u[:, bank, q:HALF],
                                 both(v, slice(None), j, slice(pr * D, pr * D + D)),
                                 both(p_t, slice(None), slice(at + q, at + HALF)),
                                 j == 0, j == tiles - 1)
                if j == tiles - 1:
                    last.then_inc(unit_done, 1)

            def project_out(bank, c):
                for t in (2 * c, 2 * c + 1):
                    for pr in range(2):
                        last = three(ps_u[:, bank, (t % 2) * HID:(t % 2 + 1) * HID],
                                     both(ctx_t, slice(None), pr, slice(t * P, t * P + P)),
                                     both(o_w, slice(None), pr, slice(None)),
                                     pr == 0, pr == 1)
                last.then_inc(unit_done, 1)

            def unit(n, kind, p, name):
                begin, name = name[-1] == "-", name.rstrip("-")
                bank, c = bank_of(kind, p, name), int(name[-1])
                if begin or name != "_pv1":
                    free_bank(number(n, kind, p, name))
                if "q" in name or "k" in name:
                    if name in ("q1", "nq0"):
                        head = 2 * n + p + (name[0] == "n")
                        pe.wait_ge(qk_w_hi, head + 1)
                        pe.wait_ge(qk_w_lo, head + 1)
                    if name == "q1" and kind == FIRST and p == 0:
                        pe.wait_ge(xn_lo, 4)
                    project(bank, int("k" in name), parity_of(p, name), c)
                elif "pv" in name:
                    pe.wait_ge(p_lo, groups_to(n, p, 3 if c == 0 else -1))
                    if p == 0 and c == 0:
                        pe.wait_ge(unit_used, number(n, kind, 0, "v1"))
                    if p == 1 and c == 1:
                        pe.wait_ge(unit_used, number(n, kind, 1, "v3"))
                    js = range(4) if begin or c == 0 else range(4, NT)
                    context(bank, parity_of(p, name), c, js)
                elif "v" in name:
                    if c == 0:
                        pe.wait_ge(v_w_hi, n + 1)
                        pe.wait_ge(v_w_lo, n + 1)
                    values(bank, c)
                else:
                    if c == 0:
                        pe.wait_ge(o_w_hi, n)
                        pe.wait_ge(o_w_lo, n)
                        pe.wait_ge(unit_used, number(n - 1, STEADY, 1, "pv0"))
                    if c == 2:
                        pe.wait_ge(unit_used, number(n, kind, 0, "_pv1"))
                    project_out(bank, c)

            def scores(n, kind, p, i):
                if not (kind == FIRST and p == 0 and i < 2):
                    pe.wait_ge(scores_masked, tile_no(n, p, i) - 1)
                if i in (0, 4):
                    if i == 4:
                        pe.wait_ge(unit_used, number(n, kind, p, "k1"))
                    elif p == 1:
                        pe.wait_ge(unit_used, number(n, kind, 0, "nk0"))
                    elif kind == FIRST:
                        pe.wait_ge(unit_used, 2)
                    else:
                        pe.wait_ge(unit_used, number(n - 1, STEADY, 1, "nk0"))
                width = (i + 1) * P
                for at in range(0, width, HALF):
                    to = max(min(width, at + HALF), at + 2 * P)
                    last = three(ps_s[:, i % 2, at:to],
                                 both(qk, slice(None), p, 0, slice(i * P, i * P + P)),
                                 both(qk, slice(None), p, 1, slice(at, to)), True, True)
                last.then_inc(scores_done, 1)

            def turn(n, p, i, back):
                pe.wait_ge(normed, tile_no(n, p, i - NT if back else i) + 1)
                for g in range(GROUPS[i]):
                    room = (GROUPS_BEFORE[i] + g) % 2
                    no = groups_to(n, p, i - NT - 1 if back else i - 1) + g + 1
                    if not (isinstance(no, int) and no <= 2):
                        pe.wait_ge(p_lo, no - 2)
                    for b, j in enumerate(turned(i, g)):
                        last = pe.transpose(ps_t[:, room, b * P:(b + 1) * P],
                                            slot(i)[:, j * P:(j + 1) * P], ident[:, :])
                    last.then_inc(p_turned, 1)

            def turn_x(c):
                pe.wait_ge(xn_ready, 4 * c + 4)
                for kk in range(KT):
                    for t in range(4 * c, 4 * c + 4):
                        last = pe.transpose(ps_s[:, kk, t * P:(t + 1) * P], xn[:, t, kk * P:(kk + 1) * P],
                                            ident[:, :])
                    last.then_inc(xn_turned, 1)

            pe.wait_ge(made, 2)
            turn_x(0)
            pe.wait_ge(xn_lo, 2)
            pe.wait_ge(qk_w_hi, 1)
            pe.wait_ge(qk_w_lo, 1)
            project(0, 0, 0, 0)
            project(1, 1, 0, 0)
            turn_x(1)

            def pair(n, kind):
                for p in range(2):
                    for i in range(NT):
                        scores(n, kind, p, i)
                        t = lagged(kind, p, i)
                        if t is not None:
                            turn(n, p, t, i < LAG)
                        for name, step in units_of(kind, p, True):
                            if step == i:
                                unit(n, kind, p, name)

            all_pairs(pe, pair)

            def gate_up(u):
                f, c = u % FT, u // FT
                if c == 0:
                    pe.wait_ge(ffn_w_lo, f + 1)
                if u < 2:
                    pe.wait_ge(scores_masked, HEADS * NT - 1 + u)
                else:
                    pe.wait_ge(h_ready, u - 1)
                for which in range(2):
                    for kk in range(KT):
                        at = (which * KT + kk) * P
                        last = three(ps_s[:, u % 2, which * HALF:(which + 1) * HALF],
                                     [ffn_w(0, f, at, P), ffn_w(1, f, at, P)],
                                     both(xn_t, slice(None), kk, slice(c * HALF, c * HALF + HALF)),
                                     kk == 0, kk == KT - 1)
                last.then_inc(gate_up_done, 1)

            units = number(PAIRS - 1, LAST, 1, "pv0")
            for what, no in TAIL:
                if what == "turn":
                    turn(PAIRS, 0, no, True)
                elif what == "gate_up":
                    gate_up(no)
                elif what == "pv":
                    pe.wait_ge(p_lo, HEADS * HEAD_GROUPS)
                    units += 1
                    free_bank(units)
                    context((units - 1) % 2, 1, 1, range(NT))
                else:
                    if no == 0:
                        pe.wait_ge(o_w_hi, PAIRS)
                        pe.wait_ge(o_w_lo, PAIRS)
                    if no in (0, 2):
                        pe.wait_ge(unit_used, units)
                    units += 1
                    free_bank(units)
                    project_out((units - 1) % 2, no)
            pe.wait_ge(ffn_w_lo, PIECES)
            pe.wait_ge(p_lo, HEADS * HEAD_GROUPS)
            for d in range(NT // 2):
                if d >= 2:
                    pe.wait_ge(out_ready, d - 1)
                c = d // 2
                pe.wait_ge(h_lo_done, (c + 1) * FT)
                for t in range(2):
                    q = ((2 * d + t) % 4) * P
                    for f in range(FT):
                        u, piece, at = c * FT + f, FT + f // 2, (f % 2) * HID
                        last = three(ps_t[:, d % 2, t * HID:(t + 1) * HID],
                                     [h_tile(0, u)[:, q:q + P], h_tile(1, u)[:, q:q + P]],
                                     [ffn_w(0, piece, at, HID), ffn_w(1, piece, at, HID)], f == 0, f == FT - 1)
                last.then_inc(down_done, 1)

        @block.scalar
        def _(act):
            def root(c):
                act.wait_ge(ln_step, 8 * c + 3)
                act.activation(ln[:, 1, 4 * c:4 * c + 4], ln[:, 0, 4 * c:4 * c + 4],
                               ACT.Sqrt).then_inc(root_done, 1)

            def xn_hi_of(c):
                for kk in range(KT):
                    act.wait_ge(xn_turned, KT * c + kk + 1)
                    act.activation(xn_t[0][:, kk, c * HALF:(c + 1) * HALF],
                                   ps_s[:, kk, c * HALF:(c + 1) * HALF], ACT.Copy).then_inc(xn_hi, 1)

            root(0)
            act.wait_ge(qk_landed, 16)
            act.activation(qk_w[0][:, 0, :, :], qk_raw[:, :, :], ACT.Copy).then_inc(qk_w_hi, 1)
            xn_hi_of(0)
            root(1)

            def hi_of(n, p, name, bank, no):
                act.wait_ge(unit_done, no)
                b = unit_bias(p, name)
                if b is None:
                    act.activation(unit_place(0, p, name), ps_u[:, bank, :], ACT.Copy).then_inc(unit_hi, 1)
                else:
                    act.activation(unit_place(0, p, name), ps_u[:, bank, :], ACT.Identity,
                                   bias=b).then_inc(unit_hi, 1)

            act.wait_ge(bias_ready, 1)
            hi_of(0, 0, "q0", 0, 1)
            hi_of(0, 0, "k0", 1, 2)
            xn_hi_of(1)
            act.wait_ge(qk_landed, 32)
            act.activation(qk_w[0][:, 1, :, :], qk_raw[:, :, :], ACT.Copy).then_inc(qk_w_hi, 1)
            act.wait_ge(v_landed, 16)
            act.activation(v_w[0][:, :, :], v_raw[:, :, :], ACT.Copy).then_inc(v_w_hi, 1)

            def exp(n, p, i):
                act.wait_ge(scores_masked, tile_no(n, p, i) + 1)
                col = p * NT + i
                act.activation(slot(i), slot(i), ACT.Exp, bias=neg_max[:, col:col + 1], scale=-1.0,
                               accum_out=row_sum[:, col:col + 1]).then_inc(exp_done, 1)

            def p_hi_of(n, p, i, back):
                for g in range(GROUPS[i]):
                    room = (GROUPS_BEFORE[i] + g) % 2
                    act.wait_ge(p_turned, groups_to(n, p, i - NT - 1 if back else i - 1) + g + 1)
                    act.activation(p_rows(0, i, g),
                                   ps_t[:, room, 0:len(turned(i, g)) * P].rearrange("p (j q) -> p j q", q=P),
                                   ACT.Copy).then_inc(p_hi, 1)

            act.wait_ge(cleared, 1)

            def pair(n, kind):
                for p in range(2):
                    for i in range(NT):
                        if i == 2 and not (kind == LAST and p == 1):
                            act.wait_ge(bias_ready, 4 * n + 2 * p + 2)
                        if i == 6:
                            act.wait_ge(bias_ready, 4 * n + 2 * p + 1)
                        t = lagged(kind, p, i)
                        if t is not None:
                            p_hi_of(n, p, t, i < LAG)
                        for name, step in units_of(kind, p):
                            if step == i and is_split(name):
                                hi_of(n, p, name, bank_of(kind, p, name), number(n, kind, p, name))
                        exp(n, p, i)
                        if i == 4 and kind != LAST:
                            act.wait_ge(qk_landed, n * 32 + (p + 3) * 16)
                            act.wait_ge(unit_done, number(n, kind, p, "k1"))
                            act.activation(qk_w[0][:, p, :, :], qk_raw[:, :, :], ACT.Copy).then_inc(qk_w_hi, 1)
                        if i == 2 and p == 1 and kind != LAST:
                            act.wait_ge(v_landed, n * 16 + 32)
                            act.wait_ge(unit_done, number(n, kind, 1, "v3"))
                            act.activation(v_w[0][:, :, :], v_raw[:, :, :], ACT.Copy).then_inc(v_w_hi, 1)
                        if i == 6 and p == 1:
                            act.wait_ge(o_landed, n * 16 + 16)
                            if kind != FIRST:
                                act.wait_ge(unit_done, number(n, kind, 1, "_out3"))
                            act.activation(o_w[0][:, :, :], o_raw[:, :, :], ACT.Copy).then_inc(o_w_hi, 1)

                        if 3 <= i < 7 and kind == LAST and p == 1:
                            ffn_w_hi_of(i - 3)

            def ffn_w_hi_of(piece):
                reached = -(-(piece + 1) * PIECE // LUT_PIECE)
                act.wait_ge(term_added, (HEADS - 2) * TERMS + reached)
                act.activation(ffn_w(0, piece), w_ffn[:, piece * PIECE:(piece + 1) * PIECE],
                               ACT.Copy).then_inc(ffn_w_hi, 1)

            all_pairs(act, pair)

            def hidden(u):
                act.wait_ge(gate_up_done, u + 1)
                if u < 2:
                    act.wait_ge(term_added, (HEADS - 1) * TERMS)
                else:
                    act.wait_ge(h_ready, u - 1)
                act.activation(silu_tile(u), ps_s[:, u % 2, 0:HALF], ACT.Silu).then_inc(silu_done, 1)
                act.wait_ge(h_ready, u + 1)
                act.activation(h_tile(0, u), h_raw(u), ACT.Copy).then_inc(h_hi_done, 1)

            units = number(PAIRS - 1, LAST, 1, "pv0")
            for what, no in TAIL:
                if what == "turn":
                    p_hi_of(PAIRS, 0, no, True)
                elif what == "gate_up":
                    hidden(no)
                    if 3 <= no < PIECES - 3:
                        ffn_w_hi_of(no + 3)
                else:
                    units += 1
                    if what == "pv":
                        hi_of(PAIRS, 0, "_pv1", (units - 1) % 2, units)
                        ffn_w_hi_of(4)
                        ffn_w_hi_of(5)

        @block.vector
        def _(dve):
            def statistics(c):
                tiles, at = range(4 * c, 4 * c + 4), slice(4 * c, 4 * c + 4)
                var, root, inv, aux = ln[:, 0, at], ln[:, 1, at], ln[:, 2, at], ln[:, 3, at]
                dve.wait_ge(x_landed[c], 16)
                for t in tiles:
                    last = dve.bn_stats(stats[:, t, :], acc[:, t, :])
                last.then_inc(ln_step, 1)
                dve.wait_ge(ln_step, 8 * c + 1)
                for t in tiles:
                    last = dve.bn_aggr(moments[:, t, :], stats[:, t, :])
                last.then_inc(ln_step, 1)
                dve.wait_ge(ln_step, 8 * c + 2)
                dve.tensor_scalar(var, moments[:, at, 1], EPS, None, ALU.add).then_inc(ln_step, 1)
                dve.wait_ge(root_done, c + 1)
                dve.reciprocal(inv, root).then_inc(ln_step, 1)
                dve.wait_ge(ln_step, 8 * c + 4)
                dve.tensor_tensor(aux, inv, inv, ALU.mult).then_inc(ln_step, 1)
                dve.wait_ge(ln_step, 8 * c + 5)
                dve.tensor_tensor(aux, aux, var, ALU.mult).then_inc(ln_step, 1)
                dve.wait_ge(ln_step, 8 * c + 6)
                dve.tensor_scalar(aux, aux, -0.5, 1.5, ALU.mult, ALU.add).then_inc(ln_step, 1)
                dve.wait_ge(ln_step, 8 * c + 7)
                dve.tensor_tensor(inv, inv, aux, ALU.mult).then_inc(ln_step, 1)
                dve.wait_ge(ln_step, 8 * c + 8)

            def normalise(c):
                for t in range(4 * c, 4 * c + 4):
                    dve.tensor_scalar(xn[:, t, :], acc[:, t, :], moments[:, t, 0:1], ln[:, 2, t:t + 1],
                                      ALU.subtract, ALU.mult).then_inc(xn_ready, 1)

            def xn_lo_of(c):
                at = slice(c * HALF, (c + 1) * HALF)
                for kk in range(KT):
                    dve.wait_ge(xn_hi, KT * c + kk + 1)
                    dve.tensor_tensor(xn_t[1][:, kk, at], ps_s[:, kk, at], xn_t[0][:, kk, at].bitcast(F32),
                                      ALU.subtract).then_inc(xn_lo, 1)

            statistics(0)
            normalise(0)
            xn_lo_of(0)
            statistics(1)
            normalise(1)
            zero0, zero1 = pt_at(0, 3) + 2 * P, pt_at(1, 7) + 2 * P
            for part in range(2):
                dve.memset(p_t[part][:, zero0:zero0 + P].bitcast(F32), 0.0)
                last = dve.memset(p_t[part][:, zero1:zero1 + P].bitcast(F32), 0.0)
            last.then_inc(cleared, 1)
            def lo_of(n, p, name, bank, no):
                dve.wait_ge(unit_hi, no)
                b, hi = unit_bias(p, name), unit_place(0, p, name).bitcast(F32)
                if b is None:
                    dve.tensor_tensor(unit_place(1, p, name), ps_u[:, bank, :], hi,
                                      ALU.subtract).then_inc(unit_used, 1)
                else:
                    dve.scalar_tensor_tensor(unit_place(1, p, name), ps_u[:, bank, :], b, hi,
                                             ALU.add, ALU.subtract).then_inc(unit_used, 1)

            def next_bias(n, p, parity, which):
                at = slice(2 * n + p, 2 * n + p + 1) if isinstance(n, int) else bass.ds(2 * n + p, 1)
                dve.tensor_copy(bias_now[:, parity, which],
                                bias[:, at, which].rearrange("p a b -> p (a b)")).then_inc(bias_ready, 1)

            def make_alibi(n, p, parity):
                dve.tensor_scalar(alibi[:, parity, :], distance[:, :], column(slope, n, p), None,
                                  ALU.mult).then_inc(alibi_ready, 1)

            dve.wait_ge(made, 3 + LUT)
            make_alibi(0, 0, 0)
            dve.wait_ge(bias_landed, 16)
            next_bias(0, 0, 0, slice(0, 3))
            dve.wait_ge(bias_ready, 1)
            lo_of(0, 0, "q0", 0, 1)
            lo_of(0, 0, "k0", 1, 2)
            xn_lo_of(1)

            def mask(n, kind, p, i):
                dve.wait_ge(scores_done, tile_no(n, p, i) + 1)
                if i == 0:
                    dve.wait_ge(alibi_ready, 2 * n + p + 1)
                if not (kind == FIRST and p == 0 and i < 4):
                    dve.wait_ge(p_turned, groups_to(n, p, i - 4))
                width, col = (i + 1) * P, p * NT + i
                dve.memset(pad[:, col:col + 1], 0.0)
                dve.tensor_tensor_reduce(slot(i), ps_s[:, i % 2, 0:width], alibi[:, p, S - width:S],
                                         -1.0, 3.0e38, ALU.add, ALU.min,
                                         neg_max[:, col:col + 1]).then_inc(scores_masked, 1)

            def look_up(n, kind, p, part):
                piece = slice(part * LUT_PIECE, (part + 1) * LUT_PIECE)
                if kind == FIRST and p == 0:
                    dve.wait_ge(idx_landed, 16)
                    dve.tensor_copy(codes[:, piece], w_ffn[:, piece].bitcast(I32)).then_inc(codes_ready, 1)
                    dve.wait_ge(codes_ready, part + 1)
                elif kind == FIRST and part == 0:
                    dve.wait_ge(based, NT)
                else:
                    dve.wait_ge(term_added, n * (2 * TERMS) + (p - 1) * TERMS + part)
                target = w_ffn[:, piece] if kind == FIRST and p == 0 else term[:, :]
                if kind == FIRST and p == 0:
                    dve.wait_ge(small_landed, 32)
                dve.tensor_scalar(target, codes[:, piece], column(entry, n, p), column(table, n, p),
                                  ALU.is_equal, ALU.mult).then_inc(term_ready, 1)

            def invert(n, p, i):
                dve.wait_ge(exp_done, tile_no(n, p, i) + 1)
                col = (p * NT + i) % (2 * NT)
                dve.reciprocal(inv_sum[:, col:col + 1], row_sum[:, col:col + 1]).then_inc(inv_ready, 1)

            def p_lo_of(n, p, i, back):
                for g in range(GROUPS[i]):
                    room = (GROUPS_BEFORE[i] + g) % 2
                    dve.wait_ge(p_hi, groups_to(n, p, i - NT - 1 if back else i - 1) + g + 1)
                    dve.tensor_tensor(p_rows(1, i, g),
                                      ps_t[:, room, 0:len(turned(i, g)) * P].rearrange("p (j q) -> p j q", q=P),
                                      p_rows(0, i, g).bitcast(F32), ALU.subtract).then_inc(p_lo, 1)

            def add_out(c, bank, no):
                dve.wait_ge(unit_done, no)
                dve.wait_ge(unit_used, no - 1)
                dve.wait_ge(based, NT)
                rows = acc[:, 2 * c:2 * c + 2, :].rearrange("p t h -> p (t h)")
                dve.tensor_tensor(rows, ps_u[:, bank, :], rows, ALU.add).then_inc(unit_used, 1)

            def pair(n, kind):
                for p in range(2):
                    for i in range(NT):
                        mask(n, kind, p, i)
                        if not (kind == FIRST and p == 0 and i == 0):
                            invert(n, p, i - 1)
                        t = lagged(kind, p, i)
                        if t is not None:
                            p_lo_of(n, p, t, i < LAG)
                        if i == 1 and not (kind == LAST and p == 1):
                            next_bias(n, p + 1, 1 - p, slice(0, 2))
                        if i == 2 and not (kind == LAST and p == 1):
                            dve.wait_ge(bias_ready, 4 * n + 2 * p + 2)
                        if i == 5 and not (kind == LAST and p == 1):
                            if not (kind == FIRST and p == 0):
                                dve.wait_ge(unit_used, number(n, kind, p, "_pv1"))
                            next_bias(n, p + 1, 1 - p, slice(2, 3))
                        if i == 6:
                            dve.wait_ge(bias_ready, 4 * n + 2 * p + 1)
                        for name, step in units_of(kind, p):
                            if step != i:
                                continue
                            if is_split(name):
                                lo_of(n, p, name, bank_of(kind, p, name), number(n, kind, p, name, is_split))
                            else:
                                add_out(int(name[-1]), bank_of(kind, p, name), number(n, kind, p, name))
                        if i % 2 == 0:
                            look_up(n, kind, p, i // 2)
                        if i == 3 and not (kind == LAST and p == 1):
                            make_alibi(n, p + 1, 1 - p)

            all_pairs(dve, pair)

            def hidden(u):
                dve.wait_ge(silu_done, u + 1)
                if u >= 2:
                    dve.wait_ge(h_lo_done, u - 1)
                dve.tensor_tensor(h_raw(u), ps_s[:, u % 2, HALF:2 * HALF], silu_tile(u),
                                  ALU.mult).then_inc(h_ready, 1)
                dve.wait_ge(h_hi_done, u + 1)
                dve.tensor_tensor(h_tile(1, u), h_raw(u), h_tile(0, u).bitcast(F32),
                                  ALU.subtract).then_inc(h_lo_done, 1)

            invert(PAIRS, 0, -1)
            units = number(PAIRS - 1, LAST, 1, "pv0")
            for what, no in TAIL:
                if what == "turn":
                    p_lo_of(PAIRS, 0, no, True)
                elif what == "gate_up":
                    hidden(no)
                else:
                    units += 1
                    if what == "pv":
                        lo_of(PAIRS, 0, "_pv1", (units - 1) % 2, number(PAIRS - 1, LAST, 1, "pv0", is_split) + 1)
                    else:
                        add_out(no, (units - 1) % 2, units)
            for d in range(NT // 2):
                dve.wait_ge(down_done, d + 1)
                dve.wait_ge(unit_used, units)
                rows = acc[:, 2 * d:2 * d + 2, :].rearrange("p t h -> p (t h)")
                dve.tensor_tensor(rows, ps_t[:, d % 2, :], rows, ALU.add).then_inc(out_ready, 1)

        @block.gpsimd
        def _(pool):
            pool.memset(ident[:, :], 0.0).then_inc(made, 1)
            pool.wait_ge(made, 1)
            pool.affine_select(out=ident[:, :], in_=ident[:, :], compare_op=ALU.not_equal, fill=1.0, base=0,
                               pattern=[[-1, P]], channel_multiplier=1).then_inc(made, 1)
            pool.iota(distance[:, :], pattern=[[1, S]], base=-(S - P), channel_multiplier=-1,
                      allow_small_or_imprecise_dtypes=True).then_inc(iota_done, 1)
            pool.wait_ge(iota_done, 1)
            pool.affine_select(out=distance[:, :], in_=distance[:, :], compare_op=ALU.is_ge, fill=MASKED,
                               base=S - P, pattern=[[-1, S]], channel_multiplier=1).then_inc(made, 1)
            for h in range(HEADS):
                pool.memset(slope[:, h:h + 1], 1.0 / 2.0 ** (h / 2.0)).then_inc(made, 1)
            pool.iota(entry[:, :], pattern=[[1, LUT]], base=0, channel_multiplier=0,
                      allow_small_or_imprecise_dtypes=True).then_inc(made, 1)

            def qk_lo(no, parity):
                pool.wait_ge(qk_w_hi, no)
                pool.tensor_tensor(qk_w[1][:, parity, :, :], qk_raw[:, :, :], qk_w[0][:, parity, :, :].bitcast(F32),
                                   ALU.subtract).then_inc(qk_w_lo, 1)

            def v_lo(no):
                pool.wait_ge(v_w_hi, no)
                pool.tensor_tensor(v_w[1][:, :, :], v_raw[:, :, :], v_w[0][:, :, :].bitcast(F32),
                                   ALU.subtract).then_inc(v_w_lo, 1)

            qk_lo(1, 0)
            qk_lo(2, 1)
            v_lo(1)
            pool.wait_ge(xn_ready, NT)
            pool.wait_ge(small_landed, 32)

            def norm(n, p, i):
                pool.wait_ge(inv_ready, tile_no(n, p, i) + 1)
                col = (p * NT + i) % (2 * NT)
                pool.tensor_tensor(pad[:, 2 * NT + col:2 * NT + col + 1], entry[:, 0:1], entry[:, 0:1], ALU.add)
                pool.tensor_scalar(slot(i % NT), slot(i % NT), inv_sum[:, col:col + 1], 1.0, ALU.mult,
                                   ALU.mult).then_inc(normed, 1)

            def pair(n, kind):
                for p in range(2):
                    for i in range(NT):
                        if not (kind == FIRST and p == 0 and i == 0):
                            norm(n, p, i - 1)
                        if i == 4 and kind != LAST:
                            qk_lo(2 * n + p + 3, p)
                        if i == 2 and p == 1 and kind != LAST:
                            v_lo(n + 2)
                        if i == 6 and p == 1:
                            pool.wait_ge(o_w_hi, n + 1)
                            pool.tensor_tensor(o_w[1][:, :, :], o_raw[:, :, :], o_w[0][:, :, :].bitcast(F32),
                                               ALU.subtract).then_inc(o_w_lo, 1)
                        if kind == FIRST and p == 0:
                            pool.tensor_tensor(acc[:, i, :], acc[:, i, :], term[:, 0:HID],
                                               ALU.add).then_inc(based, 1)
                        elif i % 2 == 1:
                            part = i // 2
                            pool.wait_ge(term_ready, n * (2 * TERMS) + p * TERMS + part + 1)
                            if kind != FIRST:
                                pool.wait_ge(term_added, n * (2 * TERMS) + (p - 2) * TERMS + part + 1)
                            piece = w_ffn[:, part * LUT_PIECE:(part + 1) * LUT_PIECE]
                            pool.tensor_tensor(piece, piece, term[:, :], ALU.add).then_inc(term_added, 1)
                        if 3 <= i < 7 and kind == LAST and p == 1:
                            ffn_lo(i - 3)

            def ffn_lo(piece):
                pool.wait_ge(ffn_w_hi, piece + 1)
                pool.tensor_tensor(ffn_w(1, piece), w_ffn[:, piece * PIECE:(piece + 1) * PIECE],
                                   ffn_w(0, piece).bitcast(F32), ALU.subtract).then_inc(ffn_w_lo, 1)

            all_pairs(pool, pair)
            norm(PAIRS, 0, -1)

            for piece in range(4, PIECES):
                ffn_lo(piece)


def kernel(**inputs):
    import numpy as np
    import concourse.bacc as bacc
    from concourse.bass_utils import run_bass_kernel_spmd

    def heads(w, per):
        return w.reshape(KT, P, HEADS // per, per * D).transpose(2, 1, 0, 3)

    w = np.asarray(inputs["L0_attn_qkv_w"]).reshape(HID, 3, HEADS * D)
    w_qk = np.concatenate([heads(w[:, 0], 1), heads(w[:, 1], 1)], axis=3)
    w_v = heads(w[:, 2], 2)
    w_o = np.asarray(inputs["L0_attn_out_w"]).reshape(PAIRS, 2, D, HID).transpose(0, 2, 1, 3)
    b_qkv = np.asarray(inputs["L0_attn_qkv_b"]).reshape(3, HEADS, D).transpose(2, 1, 0)

    pad = ((0, FT * P - INTER), (0, 0))
    gate, up = (np.pad(np.asarray(inputs[f"L0_ffn_{s}_idx"]), pad, constant_values=LUT)
                .reshape(FT, P, KT, P).transpose(3, 0, 2, 1) for s in ("gate", "up"))
    down = np.pad(np.asarray(inputs["L0_ffn_down_idx"]).T, pad, constant_values=LUT)
    idx = np.concatenate([np.stack([gate, up], axis=2).reshape(P, FT * PIECE),
                          down.reshape(FT, P, HID).transpose(1, 0, 2).reshape(P, FT * HID)], axis=1)
    arrays = {
        "x": np.asarray(inputs["L0_attn_x"]).reshape(S, HID), "w_qk": w_qk, "w_v": w_v, "w_o": w_o,
        "b_qkv": b_qkv, "b_out": np.asarray(inputs["L0_attn_out_b"]),
        "lut": np.asarray(inputs["L0_ffn_lut"]), "idx": idx,
    }
    arrays = {name: np.ascontiguousarray(a) for name, a in arrays.items()}
    nc = bacc.Bacc("TRN2", target_bir_lowering=False, num_devices=1)
    args = [nc.dram_tensor(name, a.shape, mybir.dt.from_np(a.dtype), kind="ExternalInput").ap()
            for name, a in arrays.items()]
    out = nc.dram_tensor("out", (S, HID), F32, kind="ExternalOutput").ap()
    block_ffn(nc, *args, out)
    r = run_bass_kernel_spmd(nc, [arrays], core_ids=[0])
    return r.results[0]["out"].reshape(1, S, HID)
```

```python
from contextlib import ExitStack

import concourse.bass as bass
from concourse import mybir

ALU = mybir.AluOpType
ACT = mybir.ActivationFunctionType
F32 = mybir.dt.float32
F32R = mybir.dt.float32r
I32 = mybir.dt.int32
U8 = mybir.dt.uint8

P = 128
S, HID, HEADS, D = 1024, 256, 16, 128
INTER, LUT = 688, 16
EPS = 1e-5
KT = HID // P
NT = S // P
HALF = 512
PAIRS = HEADS // 2
FT = -(-INTER // P)
MASKED = -1.0e38
X_LOADS = slice(0, 2), slice(2, 4), slice(4, NT)
LN_STEPS = 6
WARM_UP = 22
QK_W_AT = 4
V_W_AT = 2
O_W_AT = 6
ALIBI_AT = 3
TERM_AT = 0
SUM_AT = 1
LAG = 3

GROUPS = [-(-(i + 1) // 4) for i in range(NT)]
GROUPS_BEFORE = [sum(GROUPS[:i]) for i in range(NT + 1)]
HEAD_GROUPS = GROUPS_BEFORE[NT]

SLOT_W = [(i + 5) * P for i in range(4)]
SLOT_AT = [sum(SLOT_W[:i]) for i in range(4)]

PT_TIGHT, PT_ROW = 384, HALF
PT_HALF0 = 3 * PT_TIGHT + HALF
PT_WIDE = 2 * PT_HALF0
PT_COLS = PT_WIDE + 4 * PT_ROW

REST = INTER - (FT - 1) * P
UP_AT = -(-REST // 32) * 32
PIECE = 4 * P
DOWN_AT = (FT - 1) * PIECE + KT * P
WF = DOWN_AT + FT * HID
PIECES = -(-WF // PIECE)
TERMS = 4
LUT_PIECE = WF // TERMS


def pt_at(half, j):
    if half == 0:
        return PT_HALF0 + j * PT_TIGHT
    return PT_WIDE + j * PT_ROW if j < 4 else (j - 4) * PT_TIGHT


def pt_from(half, j):
    return min(max(0, j - 4 * half) * P, 2 * P)


FIRST, STEADY, LAST = "first", "steady", "last"
UNITS = {
    FIRST: [
        (("q1", -1), ("k1", 1), ("nq0", 2), ("v0", 3), ("nk0", 4), ("v1", 4), ("v2", 6), ("pv0", 7)),
        (("q1", 0), ("k1", 1), ("v3", 2), ("_pv1-", 4), ("_pv1", 4), ("nq0", 6), ("nk0", 6), ("pv0", 7)),
    ],
    STEADY: [
        (("q1", 0), ("_out0", 0), ("k1", 1), ("_out1", 1), ("nq0", 2), ("_pv1-", 3), ("_pv1", 4),
         ("v0", 5), ("v1", 6), ("nk0", 6), ("pv0", 7), ("v2", 7)),
        (("k1", 0), ("q1", 0), ("v3", 1), ("_out2", 1), ("_out3", 2), ("_pv1-", 4), ("_pv1", 4),
         ("nk0", 6), ("nq0", 6), ("pv0", 7)),
    ],
    LAST: [
        (("q1", 0), ("k1", 1), ("_out0", 2), ("nq0", 2), ("_out1", 3), ("_pv1-", 3), ("_pv1", 3),
         ("v0", 3), ("v1", 5), ("nk0", 6), ("v2", 7), ("pv0", 7)),
        (("k1", 0), ("_out2", 0), ("q1", 1), ("_out3", 2), ("v3", 3), ("_pv1-", 5), ("_pv1", 5), ("pv0", 7)),
    ],
}
TAIL = (("turn", 5), ("gate_up", 0), ("out", 0), ("out", 1), ("turn", 6), ("gate_up", 1), ("turn", 7),
        ("gate_up", 2), ("pv", 1), ("gate_up", 3), ("out", 2), ("gate_up", 4), ("gate_up", 5),
        ("out", 3), ("gate_up", 6), ("gate_up", 7), ("gate_up", 8), ("gate_up", 9), ("gate_up", 10),
        ("gate_up", 11))


def units_of(kind, p, begun=False):
    return [(name, step) for name, step in UNITS[kind][p] if begun or name[-1] != "-"]


def is_split(name):
    return "out" not in name


def counted(kind, only):
    return [(p, name) for p in range(2) for name, _ in units_of(kind, p) if only(name)]


def number(n, kind, p, name, only=lambda name: True):
    here = counted(kind, only).index((p, name)) + 1
    per = len(counted(STEADY, only))
    return n * per + 2 + here - (0 if kind == FIRST else per - len(counted(FIRST, only)))


def last_of(n, kind, p, *names):
    names = [name for name, _ in units_of(kind, p) if name in names]
    return number(n, kind, p, names[-1])


def banks_of(i):
    banks = -(-(i + 1) * P // HALF)
    return banks, (i + 1) * P // banks


def bank_of(kind, p, name):
    return (number(0 if kind == FIRST else 2, kind, p, name) - 1) % 2


def block_ffn(nc, x, w_qk, w_v, w_o, b_qkv, b_out, lut, idx, out):
    with ExitStack() as ctx:
        def sb(name, shape, dt=F32):
            return ctx.enter_context(nc.sbuf_tensor(name, shape, dt))

        def sem(name):
            return ctx.enter_context(nc.semaphore(name))

        acc = sb("acc", [P, NT, HID])
        work = sb("work", [P, sum(SLOT_W)])
        xn_t = [sb(f"xn_t_{s}", [P, KT, S], F32R) for s in ("hi", "lo")]
        qk = [sb(f"qk_{s}", [P, 2, 2, S], F32R) for s in ("hi", "lo")]
        v = [sb(f"v_{s}", [P, NT, 2 * D], F32R) for s in ("hi", "lo")]
        p_t = [sb(f"p_t_{s}", [P, PT_COLS], F32R) for s in ("hi", "lo")]
        ctx_t = [sb(f"ctx_t_{s}", [P, 2, S], F32R) for s in ("hi", "lo")]
        qk_raw = sb("qk_raw", [P, KT, 2 * D])
        qk_w = [sb(f"qk_w_{s}", [P, 2, KT, 2 * D], F32R) for s in ("hi", "lo")]
        v_raw = sb("v_raw", [P, KT, 2 * D])
        v_w = [sb(f"v_w_{s}", [P, KT, 2 * D], F32R) for s in ("hi", "lo")]
        o_raw = sb("o_raw", [P, 2, HID])
        o_w = [sb(f"o_w_{s}", [P, 2, HID], F32R) for s in ("hi", "lo")]
        distance = sb("distance", [P, S])
        alibi = sb("alibi", [P, 2, S])
        codes = sb("codes", [P, WF], U8)
        w_ffn = sb("w_ffn", [P, WF])
        term = sb("term", [P, LUT_PIECE])
        ident = sb("ident", [P, P])
        bias = sb("bias", [P, HEADS, 3])
        bias_now = sb("bias_now", [P, 2, 3])
        table = sb("table", [P, LUT])
        entry = sb("entry", [P, LUT])
        slope = sb("slope", [P, HEADS])
        pad = sb("pad", [P, 4 * NT + 1])
        neg_max = sb("neg_max", [P, 2 * NT])
        row_sum = sb("row_sum", [P, 2 * NT])
        inv_sum = sb("inv_sum", [P, 2 * NT])
        stats = sb("stats", [P, NT, 6])
        moments = sb("moments", [P, NT, 2])
        ln = sb("ln", [P, 3, NT])
        eps = sb("eps", [P, 1])

        ps_s = ctx.enter_context(nc.psum_tensor("ps_s", [P, 2, S], F32))
        ps_t = ctx.enter_context(nc.psum_tensor("ps_t", [P, 2, HALF], F32))
        ps_u = ctx.enter_context(nc.psum_tensor("ps_u", [P, 2, HALF], F32))

        x_landed = [sem(f"x{load}_landed") for load in range(len(X_LOADS))]
        bias_landed, small_landed = sem("bias_landed"), sem("small_landed")
        idx_landed, qk_landed = sem("idx_landed"), sem("qk_landed")
        v_landed, o_landed, stored = sem("v_landed"), sem("o_landed"), sem("stored")
        xn_turned, scores_done, p_turned = sem("xn_turned"), sem("scores_done"), sem("p_turned")
        unit_done, gate_up_done, down_done = sem("unit_done"), sem("gate_up_done"), sem("down_done")
        root_done, xn_hi, exp_done, p_hi = sem("root_done"), sem("xn_hi"), sem("exp_done"), sem("p_hi")
        unit_hi, qk_w_hi, v_w_hi, o_w_hi = sem("unit_hi"), sem("qk_w_hi"), sem("v_w_hi"), sem("o_w_hi")
        ffn_w_hi, silu_done, h_hi_done = sem("ffn_w_hi"), sem("silu_done"), sem("h_hi_done")
        ln_step, xn_ready, xn_lo = sem("ln_step"), sem("xn_ready"), sem("xn_lo")
        bias_ready = sem("bias_ready")
        cleared, codes_ready, alibi_ready = sem("cleared"), sem("codes_ready"), sem("alibi_ready")
        scores_masked, inv_ready, p_lo = sem("scores_masked"), sem("inv_ready"), sem("p_lo")
        unit_used, term_ready = sem("unit_used"), sem("term_ready")
        h_ready, h_lo_done, out_ready = sem("h_ready"), sem("h_lo_done"), sem("out_ready")
        based = sem("based")
        iota_done, made, normed, term_added = sem("iota_done"), sem("made"), sem("normed"), sem("term_added")
        qk_w_lo, v_w_lo, o_w_lo, ffn_w_lo = sem("qk_w_lo"), sem("v_w_lo"), sem("o_w_lo"), sem("ffn_w_lo")

        block = ctx.enter_context(nc.Block())

        xn = work[:, 0:NT * HID].rearrange("p (t h) -> p t h", t=NT)

        def slot(i, width=None):
            at = SLOT_AT[i % 4]
            return work[:, at:at + (width or (i + 1) * P)]

        def turned(i, g):
            return range(4 * g, min(4 * g + 4, i + 1))

        def p_rows(part, i, g):
            half, js = i // 4, turned(i, g)
            at, step = pt_at(half, js[0]), (PT_ROW if half and g == 0 else PT_TIGHT)
            q = (i % 4) * P
            if step == PT_ROW:
                rows = p_t[part][:, at:at + 4 * step].rearrange("p (j q) -> p j q", q=step)
                return rows[:, 0:len(js), q:q + P]
            rows = p_t[part][:, at + q:at + q + len(js) * step].rearrange("p (j q) -> p j q", q=step)
            return rows[:, :, 0:P]

        def tile_no(n, p, i):
            return n * (2 * NT) + p * NT + i

        def groups_to(n, p, i):
            if i < 0:
                return n * (2 * HEAD_GROUPS) + (p - 1) * HEAD_GROUPS + GROUPS_BEFORE[i + NT + 1]
            return n * (2 * HEAD_GROUPS) + p * HEAD_GROUPS + GROUPS_BEFORE[i + 1]

        def lagged(kind, p, i):
            if i >= LAG:
                return i - LAG
            return None if kind == FIRST and p == 0 else i - LAG + NT

        def parity_of(p, name):
            return 1 - p if name[0] in "n_" else p

        def unit_place(part, p, name):
            pr, c = parity_of(p, name), int(name[-1])
            if "q" in name or "k" in name:
                return qk[part][:, pr, int("k" in name), c * HALF:(c + 1) * HALF]
            if "pv" in name:
                return ctx_t[part][:, pr, c * HALF:(c + 1) * HALF]
            return v[part][:, 2 * c:2 * c + 2, :].rearrange("p t d -> p (t d)")

        def unit_bias(p, name):
            if "pv" not in name and "v" in name:
                return None
            which = 2 if "pv" in name else int("k" in name)
            return bias_now[:, parity_of(p, name), which:which + 1]

        def column(tensor, n, p):
            if isinstance(n, int):
                return tensor[:, 2 * n + p:2 * n + p + 1]
            return tensor[:, bass.ds(2 * n + p, 1)]

        def ffn_w(part, at, width):
            piece, in_piece = at // PIECE, at % PIECE
            if piece < 4:
                in_piece += (piece % 2) * PIECE
                return qk[part][:, 0, piece // 2, in_piece:in_piece + width]
            in_piece += (piece - 4) * PIECE
            return p_t[part][:, in_piece:in_piece + width]

        def piece_of(piece):
            return piece * PIECE, min(PIECE, WF - piece * PIECE)

        def rows_of(u):
            return slice(0, P if u % FT < FT - 1 else REST)

        def h_tile(part, u):
            at = (u % 4) * HALF
            room = (qk[part][:, 1, :, :], v[part][:, :, :], ctx_t[part][:, :, :])[u // 4]
            return room.rearrange("p a b -> p (a b)")[:, at:at + HALF]

        def silu_tile(u):
            return term[:, (u % 2) * HALF:(u % 2 + 1) * HALF]

        def h_raw(u):
            return alibi[:, 0, (u % 2) * HALF:(u % 2 + 1) * HALF]

        def all_pairs(engine, pair):
            pair(0, FIRST)
            with engine.Fori(1, PAIRS - 1) as n:
                pair(n, STEADY)
            pair(PAIRS - 1, LAST)

        @block.sync
        def _(sp):
            x_t = x.rearrange("(t p) h -> p t h", p=P)
            for load, tiles in enumerate(X_LOADS):
                sp.dma_start(acc[:, tiles, :], x_t[:, tiles, :]).then_inc(x_landed[load], 16)
            sp.dma_start(qk_raw[:, :, :], w_qk[0]).then_inc(qk_landed, 16)
            sp.dma_start(bias[:, :, :], b_qkv).then_inc(bias_landed, 16)
            sp.dma_start(v_raw[:, :, :], w_v[0]).then_inc(v_landed, 16)
            sp.dma_start(table[:, :], lut.partition_broadcast(P)).then_inc(small_landed, 16)
            sp.dma_start(term[:, 0:HID], b_out.partition_broadcast(P)).then_inc(small_landed, 16)
            sp.dma_start(w_ffn[:, :].bitcast(I32), idx).then_inc(idx_landed, 16)
            sp.dma_start(o_raw[:, :, :], w_o[0]).then_inc(o_landed, 16)
            for h in (1, 2):
                sp.wait_ge(qk_w_hi, h)
                sp.wait_ge(qk_w_lo, h)
                sp.dma_start(qk_raw[:, :, :], w_qk[h]).then_inc(qk_landed, 16)
            sp.wait_ge(v_w_hi, 1)
            sp.wait_ge(v_w_lo, 1)
            sp.dma_start(v_raw[:, :, :], w_v[1]).then_inc(v_landed, 16)

            def refill(n, to_the_end):
                sp.wait_ge(qk_w_hi, n * 2 + 3)
                sp.wait_ge(qk_w_lo, n * 2 + 3)
                sp.dma_start(qk_raw[:, :, :], w_qk[n * 2 + 3]).then_inc(qk_landed, 16)
                if not to_the_end:
                    sp.wait_ge(v_w_hi, n + 2)
                    sp.wait_ge(v_w_lo, n + 2)
                    sp.dma_start(v_raw[:, :, :], w_v[n + 2]).then_inc(v_landed, 16)
                    sp.wait_ge(qk_w_hi, n * 2 + 4)
                    sp.wait_ge(qk_w_lo, n * 2 + 4)
                    sp.dma_start(qk_raw[:, :, :], w_qk[n * 2 + 4]).then_inc(qk_landed, 16)
                sp.wait_ge(o_w_hi, n + 1)
                sp.wait_ge(o_w_lo, n + 1)
                sp.dma_start(o_raw[:, :, :], w_o[n + 1]).then_inc(o_landed, 16)

            with sp.Fori(0, PAIRS - 2) as n:
                refill(n, False)
            refill(PAIRS - 2, True)
            out_t = out.rearrange("(t p) h -> p t h", p=P)
            for t in range(NT):
                sp.wait_ge(out_ready, t + 1)
                sp.dma_start(out_t[:, t, :], acc[:, t, :]).then_inc(stored, 16)
            sp.wait_ge(stored, 16 * NT)

        @block.tensor
        def _(pe):
            def three(out, lhs, rhs, first, last):
                pe.matmul(out, lhs[0], rhs[0], start=first, stop=False)
                pe.matmul(out, lhs[0], rhs[1], start=False, stop=False)
                return pe.matmul(out, lhs[1], rhs[0], start=False, stop=last)

            def both(tensor, *where):
                return [t[where] for t in tensor]

            def free_bank(no):
                if isinstance(no, int) and no <= 2:
                    return
                pe.wait_ge(unit_used, no - 2)

            def project(bank, which, pr, c):
                for kk in range(KT):
                    last = three(ps_u[:, bank, :],
                                 both(qk_w, slice(None), pr, kk, slice(which * D, which * D + D)),
                                 both(xn_t, slice(None), kk, slice(c * HALF, c * HALF + HALF)),
                                 kk == 0, kk == KT - 1)
                last.then_inc(unit_done, 1)

            def values(bank, c):
                for t in (2 * c, 2 * c + 1):
                    for kk in range(KT):
                        last = three(ps_u[:, bank, (t % 2) * 2 * D:(t % 2 + 1) * 2 * D],
                                     both(xn_t, slice(None), kk, slice(t * P, t * P + P)),
                                     both(v_w, slice(None), kk, slice(None)),
                                     kk == 0, kk == KT - 1)
                last.then_inc(unit_done, 1)

            def context(bank, pr, c, js):
                tiles = 4 * c + 4
                for j in js:
                    q, at = pt_from(c, j), pt_at(c, j)
                    last = three(ps_u[:, bank, q:HALF],
                                 both(v, slice(None), j, slice(pr * D, pr * D + D)),
                                 both(p_t, slice(None), slice(at + q, at + HALF)),
                                 j == 0, j == tiles - 1)
                if j == tiles - 1:
                    last.then_inc(unit_done, 1)

            def project_out(bank, c):
                for t in (2 * c, 2 * c + 1):
                    for pr in range(2):
                        last = three(ps_u[:, bank, (t % 2) * HID:(t % 2 + 1) * HID],
                                     both(ctx_t, slice(None), pr, slice(t * P, t * P + P)),
                                     both(o_w, slice(None), pr, slice(None)),
                                     pr == 0, pr == 1)
                last.then_inc(unit_done, 1)

            def unit(n, kind, p, name):
                begin, name = name[-1] == "-", name.rstrip("-")
                bank, c = bank_of(kind, p, name), int(name[-1])
                if begin or name != "_pv1":
                    free_bank(number(n, kind, p, name))
                if "q" in name or "k" in name:
                    head = 2 * n + p + (name[0] == "n")
                    pe.wait_ge(qk_w_hi, head + 1)
                    pe.wait_ge(qk_w_lo, head + 1)
                    if name == "q1" and kind == FIRST and p == 0:
                        pe.wait_ge(xn_lo, 4)
                    project(bank, int("k" in name), parity_of(p, name), c)
                elif "pv" in name:
                    pe.wait_ge(p_lo, groups_to(n, p, 3 if c == 0 else -1))
                    if p == 0 and c == 0:
                        pe.wait_ge(unit_used, number(n, kind, 0, "v1"))
                    if p == 1 and c == 1:
                        pe.wait_ge(unit_used, number(n, kind, 1, "v3"))
                    js = range(4) if begin or c == 0 else range(4, NT)
                    context(bank, parity_of(p, name), c, js)
                elif "v" in name:
                    if c == 0:
                        pe.wait_ge(v_w_hi, n + 1)
                        pe.wait_ge(v_w_lo, n + 1)
                    values(bank, c)
                else:
                    if c == 0:
                        pe.wait_ge(o_w_hi, n)
                        pe.wait_ge(o_w_lo, n)
                        pe.wait_ge(unit_used, number(n - 1, STEADY, 1, "pv0"))
                    if c == 2:
                        pe.wait_ge(unit_used, number(n, kind, 0, "_pv1"))
                    project_out(bank, c)

            def scores(n, kind, p, i):
                if not (kind == FIRST and p == 0 and i < 2):
                    pe.wait_ge(scores_masked, tile_no(n, p, i) - 1)
                if i in (0, 4):
                    if i == 4:
                        pe.wait_ge(unit_used, last_of(n, kind, p, "q1", "k1"))
                    elif p == 1:
                        pe.wait_ge(unit_used, last_of(n, kind, 0, "nq0", "nk0"))
                    elif kind == FIRST:
                        pe.wait_ge(unit_used, 2)
                    else:
                        pe.wait_ge(unit_used, last_of(n - 1, STEADY, 1, "nq0", "nk0"))
                banks, per = banks_of(i)
                wide = max(per, 2 * P)
                for b in range(banks):
                    last = three(ps_s[:, i % 2, b * HALF:b * HALF + wide],
                                 both(qk, slice(None), p, 0, slice(i * P, i * P + P)),
                                 both(qk, slice(None), p, 1, slice(b * per, b * per + wide)), True, True)
                last.then_inc(scores_done, 1)

            def turn(n, p, i, back):
                pe.wait_ge(normed, tile_no(n, p, i - NT if back else i) + 1)
                for g in range(GROUPS[i]):
                    room = (GROUPS_BEFORE[i] + g) % 2
                    no = groups_to(n, p, i - NT - 1 if back else i - 1) + g + 1
                    if not (isinstance(no, int) and no <= 2):
                        pe.wait_ge(p_lo, no - 2)
                    for b, j in enumerate(turned(i, g)):
                        last = pe.transpose(ps_t[:, room, b * P:(b + 1) * P],
                                            slot(i)[:, j * P:(j + 1) * P], ident[:, :])
                    last.then_inc(p_turned, 1)

            def turn_x(c):
                pe.wait_ge(xn_ready, 4 * c + 4)
                for kk in range(KT):
                    for t in range(4 * c, 4 * c + 4):
                        last = pe.transpose(ps_s[:, kk, t * P:(t + 1) * P], xn[:, t, kk * P:(kk + 1) * P],
                                            ident[:, :])
                    last.then_inc(xn_turned, 1)

            def keep_warm():
                for _ in range(WARM_UP):
                    pe.transpose(ps_t[:, 0, 0:P], ident[:, :], ident[:, :])

            pe.wait_ge(made, 3)
            keep_warm()
            turn_x(0)
            keep_warm()
            pe.wait_ge(xn_lo, 2)
            pe.wait_ge(qk_w_hi, 1)
            pe.wait_ge(qk_w_lo, 1)
            project(0, 0, 0, 0)
            turn_x(1)
            project(1, 1, 0, 0)
            unit(0, FIRST, 0, "q1")

            def pair(n, kind):
                for p in range(2):
                    for i in range(NT):
                        scores(n, kind, p, i)
                        t = lagged(kind, p, i)
                        if t is not None:
                            turn(n, p, t, i < LAG)
                        for name, step in units_of(kind, p, True):
                            if step == i:
                                unit(n, kind, p, name)

            all_pairs(pe, pair)

            def gate_up(u):
                f, c = u % FT, u // FT
                if c == 0:
                    pe.wait_ge(ffn_w_lo, f + 1)
                if u < 2:
                    pe.wait_ge(scores_masked, HEADS * NT - 1 + u)
                else:
                    pe.wait_ge(h_ready, u - 1)
                for which in range(2 if f < FT - 1 else 1):
                    for kk in range(KT):
                        at = f * PIECE + (which * KT + kk) * P
                        last = three(ps_s[:, u % 2, which * HALF:(which + 1) * HALF],
                                     [ffn_w(0, at, P), ffn_w(1, at, P)],
                                     both(xn_t, slice(None), kk, slice(c * HALF, c * HALF + HALF)),
                                     kk == 0, kk == KT - 1)
                last.then_inc(gate_up_done, 1)

            units = number(PAIRS - 1, LAST, 1, "pv0")
            for what, no in TAIL:
                if what == "turn":
                    turn(PAIRS, 0, no, True)
                elif what == "gate_up":
                    gate_up(no)
                elif what == "pv":
                    pe.wait_ge(p_lo, HEADS * HEAD_GROUPS)
                    units += 1
                    free_bank(units)
                    context((units - 1) % 2, 1, 1, range(NT))
                else:
                    if no == 0:
                        pe.wait_ge(o_w_hi, PAIRS)
                        pe.wait_ge(o_w_lo, PAIRS)
                    if no in (0, 2):
                        pe.wait_ge(unit_used, units)
                    units += 1
                    free_bank(units)
                    project_out((units - 1) % 2, no)
            pe.wait_ge(ffn_w_lo, PIECES)
            pe.wait_ge(p_lo, HEADS * HEAD_GROUPS)
            for t in range(NT):
                if t >= 2:
                    pe.wait_ge(out_ready, t - 1)
                c, q = t // 4, (t % 4) * P
                pe.wait_ge(h_lo_done, (c + 1) * FT)
                for f in range(FT):
                    u, at = c * FT + f, DOWN_AT + f * HID
                    rows = rows_of(u)
                    last = three(ps_t[:, t % 2, 0:HID],
                                 [h_tile(0, u)[rows, q:q + P], h_tile(1, u)[rows, q:q + P]],
                                 [ffn_w(0, at, HID)[rows, :], ffn_w(1, at, HID)[rows, :]],
                                 f == 0, f == FT - 1)
                last.then_inc(down_done, 1)

        @block.scalar
        def _(act):
            def root(c):
                act.wait_ge(ln_step, LN_STEPS * c + 2)
                act.activation(ln[:, 0, 4 * c:4 * c + 4], moments[:, 4 * c:4 * c + 4, 1],
                               ACT.Sqrt, bias=eps[:, :]).then_inc(root_done, 1)

            def xn_hi_of(c, kks=range(KT)):
                for kk in kks:
                    act.wait_ge(xn_turned, KT * c + kk + 1)
                    act.activation(xn_t[0][:, kk, c * HALF:(c + 1) * HALF],
                                   ps_s[:, kk, c * HALF:(c + 1) * HALF], ACT.Copy).then_inc(xn_hi, 1)

            act.wait_ge(made, 1)
            act.activation(pad[:, 4 * NT:], eps[:, :], ACT.Sqrt)
            root(0)
            act.wait_ge(qk_landed, 16)
            act.activation(qk_w[0][:, 0, :, :], qk_raw[:, :, :], ACT.Copy).then_inc(qk_w_hi, 1)
            xn_hi_of(0, (0,))
            root(1)
            xn_hi_of(0, (1,))
            act.activation(pad[:, 4 * NT:], eps[:, :], ACT.Exp)

            def hi_of(n, p, name, bank, no):
                act.wait_ge(unit_done, no)
                b = unit_bias(p, name)
                if b is None:
                    act.activation(unit_place(0, p, name), ps_u[:, bank, :], ACT.Copy).then_inc(unit_hi, 1)
                else:
                    act.activation(unit_place(0, p, name), ps_u[:, bank, :], ACT.Identity,
                                   bias=b).then_inc(unit_hi, 1)

            act.wait_ge(bias_ready, 1)
            hi_of(0, 0, "q0", 0, 1)
            xn_hi_of(1)
            hi_of(0, 0, "k0", 1, 2)
            hi_of(0, 0, "q1", 0, 3)
            act.wait_ge(qk_landed, 32)
            act.activation(qk_w[0][:, 1, :, :], qk_raw[:, :, :], ACT.Copy).then_inc(qk_w_hi, 1)
            act.wait_ge(v_landed, 16)
            act.activation(v_w[0][:, :, :], v_raw[:, :, :], ACT.Copy).then_inc(v_w_hi, 1)

            def exp(n, p, i):
                act.wait_ge(scores_masked, tile_no(n, p, i) + 1)
                col = p * NT + i
                act.activation(slot(i), slot(i), ACT.Exp, bias=neg_max[:, col:col + 1], scale=-1.0,
                               accum_out=row_sum[:, col:col + 1]).then_inc(exp_done, 1)

            def p_hi_of(n, p, i, back):
                for g in range(GROUPS[i]):
                    room = (GROUPS_BEFORE[i] + g) % 2
                    act.wait_ge(p_turned, groups_to(n, p, i - NT - 1 if back else i - 1) + g + 1)
                    act.activation(p_rows(0, i, g),
                                   ps_t[:, room, 0:len(turned(i, g)) * P].rearrange("p (j q) -> p j q", q=P),
                                   ACT.Copy).then_inc(p_hi, 1)

            act.wait_ge(cleared, 1)

            def pair(n, kind):
                for p in range(2):
                    for i in range(NT):
                        if i == 2 and not (kind == LAST and p == 1):
                            act.wait_ge(bias_ready, 4 * n + 2 * p + 2)
                        if i == 6:
                            act.wait_ge(bias_ready, 4 * n + 2 * p + 1)
                        t = lagged(kind, p, i)
                        if t is not None:
                            p_hi_of(n, p, t, i < LAG)
                        for name, step in units_of(kind, p):
                            if step == i and is_split(name):
                                hi_of(n, p, name, bank_of(kind, p, name), number(n, kind, p, name))
                        exp(n, p, i)
                        if i == QK_W_AT and kind != LAST:
                            act.wait_ge(qk_landed, n * 32 + (p + 3) * 16)
                            act.wait_ge(unit_done, last_of(n, kind, p, "q1", "k1"))
                            act.activation(qk_w[0][:, p, :, :], qk_raw[:, :, :], ACT.Copy).then_inc(qk_w_hi, 1)
                        if i == V_W_AT and p == 1 and kind != LAST:
                            act.wait_ge(v_landed, n * 16 + 32)
                            act.wait_ge(unit_done, number(n, kind, 1, "v3"))
                            act.activation(v_w[0][:, :, :], v_raw[:, :, :], ACT.Copy).then_inc(v_w_hi, 1)
                        if i == O_W_AT and p == 1:
                            act.wait_ge(o_landed, n * 16 + 16)
                            if kind != FIRST:
                                act.wait_ge(unit_done, number(n, kind, 1, "_out3"))
                            act.activation(o_w[0][:, :, :], o_raw[:, :, :], ACT.Copy).then_inc(o_w_hi, 1)

                        if 3 <= i < 7 and kind == LAST and p == 1:
                            ffn_w_hi_of(i - 3)

            def ffn_w_hi_of(piece):
                at, width = piece_of(piece)
                reached = -(-(at + width) // LUT_PIECE)
                act.wait_ge(term_added, (HEADS - 2) * TERMS + reached)
                act.activation(ffn_w(0, at, width), w_ffn[:, at:at + width],
                               ACT.Copy).then_inc(ffn_w_hi, 1)

            all_pairs(act, pair)

            def silu_of(u):
                act.wait_ge(gate_up_done, u + 1)
                if u < 2:
                    act.wait_ge(term_added, (HEADS - 1) * TERMS)
                else:
                    act.wait_ge(h_ready, u - 1)
                rows = rows_of(u)
                act.activation(silu_tile(u)[rows, :], ps_s[rows, u % 2, 0:HALF], ACT.Silu).then_inc(silu_done, 1)

            def h_hi_of(u):
                rows = rows_of(u)
                act.wait_ge(h_ready, u + 1)
                act.activation(h_tile(0, u)[rows, :], h_raw(u)[rows, :], ACT.Copy).then_inc(h_hi_done, 1)

            act.activation(pad[:, 4 * NT:], eps[:, :], ACT.Silu)
            units = number(PAIRS - 1, LAST, 1, "pv0")
            for what, no in TAIL:
                if what == "turn":
                    p_hi_of(PAIRS, 0, no, True)
                elif what == "gate_up":
                    silu_of(no)
                    if no > 0:
                        h_hi_of(no - 1)
                    if 3 <= no < PIECES - 3:
                        ffn_w_hi_of(no + 3)
                else:
                    units += 1
                    if what == "pv":
                        hi_of(PAIRS, 0, "_pv1", (units - 1) % 2, units)
                        ffn_w_hi_of(4)
                        ffn_w_hi_of(5)
            h_hi_of(2 * FT - 1)

        @block.vector
        def _(dve):
            def statistics(c):
                tiles, at = range(4 * c, 4 * c + 4), slice(4 * c, 4 * c + 4)
                root, inv, aux = ln[:, 0, at], ln[:, 1, at], ln[:, 2, at]
                for t in tiles:
                    for load, loaded in enumerate(X_LOADS):
                        if t == loaded.start:
                            dve.wait_ge(x_landed[load], 16)
                    last = dve.bn_stats(stats[:, t, :], acc[:, t, :])
                last.then_inc(ln_step, 1)
                dve.wait_ge(ln_step, LN_STEPS * c + 1)
                for t in tiles:
                    last = dve.bn_aggr(moments[:, t, :], stats[:, t, :])
                last.then_inc(ln_step, 1)
                if c == 1:
                    xn_lo_of(0, (0,))
                dve.wait_ge(root_done, c + 1)
                dve.reciprocal(inv, root).then_inc(ln_step, 1)
                dve.wait_ge(ln_step, LN_STEPS * c + 3)
                dve.scalar_tensor_tensor(aux, inv, -0.5, inv, ALU.mult, ALU.mult).then_inc(ln_step, 1)
                dve.wait_ge(ln_step, LN_STEPS * c + 4)
                dve.scalar_tensor_tensor(aux, moments[:, at, 1], EPS, aux, ALU.add, ALU.mult).then_inc(ln_step, 1)
                dve.wait_ge(ln_step, LN_STEPS * c + 5)
                dve.scalar_tensor_tensor(inv, aux, 1.5, inv, ALU.add, ALU.mult).then_inc(ln_step, 1)
                dve.wait_ge(ln_step, LN_STEPS * c + 6)

            def normalise(c):
                for t in range(4 * c, 4 * c + 4):
                    dve.tensor_scalar(xn[:, t, :], acc[:, t, :], moments[:, t, 0:1], ln[:, 1, t:t + 1],
                                      ALU.subtract, ALU.mult).then_inc(xn_ready, 1)

            def xn_lo_of(c, kks=range(KT)):
                at = slice(c * HALF, (c + 1) * HALF)
                for kk in kks:
                    dve.wait_ge(xn_hi, KT * c + kk + 1)
                    dve.tensor_tensor(xn_t[1][:, kk, at], ps_s[:, kk, at], xn_t[0][:, kk, at].bitcast(F32),
                                      ALU.subtract).then_inc(xn_lo, 1)

            statistics(0)
            normalise(0)
            statistics(1)
            xn_lo_of(0, (1,))
            normalise(1)
            def lo_of(n, p, name, bank, no):
                dve.wait_ge(unit_hi, no)
                b, hi = unit_bias(p, name), unit_place(0, p, name).bitcast(F32)
                if b is None:
                    dve.tensor_tensor(unit_place(1, p, name), ps_u[:, bank, :], hi,
                                      ALU.subtract).then_inc(unit_used, 1)
                else:
                    dve.scalar_tensor_tensor(unit_place(1, p, name), ps_u[:, bank, :], b, hi,
                                             ALU.add, ALU.subtract).then_inc(unit_used, 1)

            def next_bias(n, p, parity, which):
                at = slice(2 * n + p, 2 * n + p + 1) if isinstance(n, int) else bass.ds(2 * n + p, 1)
                dve.tensor_copy(bias_now[:, parity, which],
                                bias[:, at, which].rearrange("p a b -> p (a b)")).then_inc(bias_ready, 1)

            def make_alibi(n, p, parity):
                dve.tensor_scalar(alibi[:, parity, :], distance[:, :], column(slope, n, p), None,
                                  ALU.mult).then_inc(alibi_ready, 1)

            dve.wait_ge(bias_landed, 16)
            next_bias(0, 0, 0, slice(0, 3))
            dve.wait_ge(made, 4 + HEADS)
            make_alibi(0, 0, 0)
            zero0, zero1 = pt_at(0, 3) + 2 * P, pt_at(1, 7) + 2 * P
            for part in range(2):
                dve.memset(p_t[part][:, zero0:zero0 + P].bitcast(F32), 0.0)
                last = dve.memset(p_t[part][:, zero1:zero1 + P].bitcast(F32), 0.0)
            last.then_inc(cleared, 1)
            dve.wait_ge(bias_ready, 1)
            lo_of(0, 0, "q0", 0, 1)
            xn_lo_of(1)
            lo_of(0, 0, "k0", 1, 2)
            lo_of(0, 0, "q1", 0, 3)

            def mask(n, kind, p, i):
                dve.wait_ge(scores_done, tile_no(n, p, i) + 1)
                if i == 0:
                    dve.wait_ge(alibi_ready, 2 * n + p + 1)
                if not (kind == FIRST and p == 0 and i < 4):
                    dve.wait_ge(p_turned, groups_to(n, p, i - 4))
                width, col = (i + 1) * P, p * NT + i
                dve.memset(pad[:, col:col + 1], 0.0)
                banks, per = banks_of(i)
                made_of = ps_s[:, i % 2, :].rearrange("p (b c) -> p b c", c=HALF)[:, 0:banks, 0:per]
                dve.tensor_tensor_reduce(slot(i).rearrange("p (b c) -> p b c", b=banks), made_of,
                                         alibi[:, p, S - width:S].rearrange("p (b c) -> p b c", b=banks),
                                         -1.0, 3.0e38, ALU.add, ALU.min,
                                         neg_max[:, col:col + 1]).then_inc(scores_masked, 1)

            def look_up(n, kind, p, part):
                piece = slice(part * LUT_PIECE, (part + 1) * LUT_PIECE)
                if kind == FIRST and p == 0:
                    dve.wait_ge(idx_landed, 16)
                    dve.tensor_copy(codes[:, piece], w_ffn[:, piece].bitcast(I32)).then_inc(codes_ready, 1)
                    dve.wait_ge(codes_ready, part + 1)
                elif kind == FIRST and part == 0:
                    dve.wait_ge(based, NT)
                else:
                    dve.wait_ge(term_added, n * (2 * TERMS) + (p - 1) * TERMS + part)
                target = w_ffn[:, piece] if kind == FIRST and p == 0 else term[:, :]
                if kind == FIRST and p == 0:
                    dve.wait_ge(small_landed, 32)
                dve.tensor_scalar(target, codes[:, piece], column(entry, n, p), column(table, n, p),
                                  ALU.is_equal, ALU.mult).then_inc(term_ready, 1)

            def invert(n, p, i):
                dve.wait_ge(exp_done, tile_no(n, p, i) + 1)
                col = (p * NT + i) % (2 * NT)
                dve.reciprocal(inv_sum[:, col:col + 1], row_sum[:, col:col + 1]).then_inc(inv_ready, 1)

            def p_lo_of(n, p, i, back):
                for g in range(GROUPS[i]):
                    room = (GROUPS_BEFORE[i] + g) % 2
                    dve.wait_ge(p_hi, groups_to(n, p, i - NT - 1 if back else i - 1) + g + 1)
                    dve.tensor_tensor(p_rows(1, i, g),
                                      ps_t[:, room, 0:len(turned(i, g)) * P].rearrange("p (j q) -> p j q", q=P),
                                      p_rows(0, i, g).bitcast(F32), ALU.subtract).then_inc(p_lo, 1)

            def add_out(c, bank, no):
                dve.wait_ge(unit_done, no)
                dve.wait_ge(unit_used, no - 1)
                dve.wait_ge(based, NT)
                rows = acc[:, 2 * c:2 * c + 2, :].rearrange("p t h -> p (t h)")
                dve.tensor_tensor(rows, ps_u[:, bank, :], rows, ALU.add).then_inc(unit_used, 1)

            def pair(n, kind):
                for p in range(2):
                    for i in range(NT):
                        last_head = kind == LAST and p == 1
                        mask(n, kind, p, i)
                        if not (kind == FIRST and p == 0 and i == 0):
                            invert(n, p, i - 1)
                        t = lagged(kind, p, i)
                        if t is not None:
                            p_lo_of(n, p, t, i < LAG)
                        if i == 1 and not last_head:
                            next_bias(n, p + 1, 1 - p, slice(0, 2))
                        if i == 2 and not last_head:
                            dve.wait_ge(bias_ready, 4 * n + 2 * p + 2)
                        if i == 5 and not last_head:
                            if not (kind == FIRST and p == 0):
                                dve.wait_ge(unit_used, number(n, kind, p, "_pv1"))
                            next_bias(n, p + 1, 1 - p, slice(2, 3))
                        if i == 6:
                            dve.wait_ge(bias_ready, 4 * n + 2 * p + 1)
                        for name, step in units_of(kind, p):
                            if step != i:
                                continue
                            if is_split(name):
                                lo_of(n, p, name, bank_of(kind, p, name), number(n, kind, p, name, is_split))
                            else:
                                add_out(int(name[-1]), bank_of(kind, p, name), number(n, kind, p, name))
                        if i % 2 == TERM_AT:
                            look_up(n, kind, p, i // 2)
                        if i == ALIBI_AT and not last_head:
                            make_alibi(n, p + 1, 1 - p)

            all_pairs(dve, pair)

            def hidden(u):
                dve.wait_ge(silu_done, u + 1)
                if u >= 2:
                    dve.wait_ge(h_lo_done, u - 1)
                rows = rows_of(u)
                up = (ps_s[:, u % 2, HALF:2 * HALF] if u % FT < FT - 1
                      else ps_s[UP_AT:UP_AT + REST, u % 2, 0:HALF])
                dve.tensor_tensor(h_raw(u)[rows, :], up, silu_tile(u)[rows, :], ALU.mult).then_inc(h_ready, 1)

            def h_lo_of(u):
                rows = rows_of(u)
                dve.wait_ge(h_hi_done, u + 1)
                dve.tensor_tensor(h_tile(1, u)[rows, :], h_raw(u)[rows, :], h_tile(0, u)[rows, :].bitcast(F32),
                                  ALU.subtract).then_inc(h_lo_done, 1)

            invert(PAIRS, 0, -1)
            units = number(PAIRS - 1, LAST, 1, "pv0")
            for what, no in TAIL:
                if what == "turn":
                    p_lo_of(PAIRS, 0, no, True)
                elif what == "gate_up":
                    hidden(no)
                    if no > 0:
                        h_lo_of(no - 1)
                else:
                    units += 1
                    if what == "pv":
                        lo_of(PAIRS, 0, "_pv1", (units - 1) % 2, number(PAIRS - 1, LAST, 1, "pv0", is_split) + 1)
                    else:
                        add_out(no, (units - 1) % 2, units)
            h_lo_of(2 * FT - 1)
            for t in range(NT):
                dve.wait_ge(down_done, t + 1)
                dve.wait_ge(unit_used, units)
                dve.tensor_tensor(acc[:, t, :], ps_t[:, t % 2, 0:HID], acc[:, t, :],
                                  ALU.add).then_inc(out_ready, 1)

        @block.gpsimd
        def _(pool):
            pool.memset(eps[:, :], EPS).then_inc(made, 1)
            pool.memset(ident[:, :], 0.0).then_inc(made, 1)
            pool.wait_ge(made, 2)
            pool.affine_select(out=ident[:, :], in_=ident[:, :], compare_op=ALU.not_equal, fill=1.0, base=0,
                               pattern=[[-1, P]], channel_multiplier=1).then_inc(made, 1)
            pool.iota(distance[:, :], pattern=[[1, S]], base=-(S - P), channel_multiplier=-1,
                      allow_small_or_imprecise_dtypes=True).then_inc(iota_done, 1)
            pool.wait_ge(iota_done, 1)
            pool.affine_select(out=distance[:, :], in_=distance[:, :], compare_op=ALU.is_ge, fill=MASKED,
                               base=S - P, pattern=[[-1, S]], channel_multiplier=1).then_inc(made, 1)
            for h in range(HEADS):
                pool.memset(slope[:, h:h + 1], 1.0 / 2.0 ** (h / 2.0)).then_inc(made, 1)
            pool.iota(entry[:, :], pattern=[[1, LUT]], base=0, channel_multiplier=0,
                      allow_small_or_imprecise_dtypes=True).then_inc(made, 1)

            def qk_lo(no, parity):
                pool.wait_ge(qk_w_hi, no)
                pool.tensor_tensor(qk_w[1][:, parity, :, :], qk_raw[:, :, :], qk_w[0][:, parity, :, :].bitcast(F32),
                                   ALU.subtract).then_inc(qk_w_lo, 1)

            def v_lo(no):
                pool.wait_ge(v_w_hi, no)
                pool.tensor_tensor(v_w[1][:, :, :], v_raw[:, :, :], v_w[0][:, :, :].bitcast(F32),
                                   ALU.subtract).then_inc(v_w_lo, 1)

            qk_lo(1, 0)
            qk_lo(2, 1)
            v_lo(1)
            pool.wait_ge(xn_ready, NT)
            pool.wait_ge(small_landed, 32)

            def norm(n, p, i):
                pool.wait_ge(inv_ready, tile_no(n, p, i) + 1)
                col = (p * NT + i) % (2 * NT)
                pool.tensor_tensor(pad[:, 2 * NT + col:2 * NT + col + 1], entry[:, 0:1], entry[:, 0:1], ALU.add)
                pool.tensor_scalar(slot(i % NT), slot(i % NT), inv_sum[:, col:col + 1], 1.0, ALU.mult,
                                   ALU.mult).then_inc(normed, 1)

            def pair(n, kind):
                for p in range(2):
                    for i in range(NT):
                        if not (kind == FIRST and p == 0 and i == 0):
                            norm(n, p, i - 1)
                        if i == QK_W_AT and kind != LAST:
                            qk_lo(2 * n + p + 3, p)
                        if i == V_W_AT and p == 1 and kind != LAST:
                            v_lo(n + 2)
                        if i == O_W_AT and p == 1:
                            pool.wait_ge(o_w_hi, n + 1)
                            pool.tensor_tensor(o_w[1][:, :, :], o_raw[:, :, :], o_w[0][:, :, :].bitcast(F32),
                                               ALU.subtract).then_inc(o_w_lo, 1)
                        if kind == FIRST and p == 0:
                            pool.tensor_tensor(acc[:, i, :], acc[:, i, :], term[:, 0:HID],
                                               ALU.add).then_inc(based, 1)
                        elif i % 2 == SUM_AT:
                            part = i // 2
                            pool.wait_ge(term_ready, n * (2 * TERMS) + p * TERMS + part + 1)
                            if kind != FIRST:
                                pool.wait_ge(term_added, n * (2 * TERMS) + (p - 2) * TERMS + part + 1)
                            piece = w_ffn[:, part * LUT_PIECE:(part + 1) * LUT_PIECE]
                            pool.tensor_tensor(piece, piece, term[:, :], ALU.add).then_inc(term_added, 1)
                        if 3 <= i < 7 and kind == LAST and p == 1:
                            ffn_lo(i - 3)

            def ffn_lo(piece):
                at, width = piece_of(piece)
                pool.wait_ge(ffn_w_hi, piece + 1)
                pool.tensor_tensor(ffn_w(1, at, width), w_ffn[:, at:at + width],
                                   ffn_w(0, at, width).bitcast(F32), ALU.subtract).then_inc(ffn_w_lo, 1)

            all_pairs(pool, pair)
            norm(PAIRS, 0, -1)

            for piece in range(4, PIECES):
                ffn_lo(piece)


def kernel(**inputs):
    import numpy as np
    import concourse.bacc as bacc
    from concourse.bass_utils import run_bass_kernel_spmd

    def heads(w, per):
        return w.reshape(KT, P, HEADS // per, per * D).transpose(2, 1, 0, 3)

    w = np.asarray(inputs["L0_attn_qkv_w"]).reshape(HID, 3, HEADS * D)
    w_qk = np.concatenate([heads(w[:, 0], 1), heads(w[:, 1], 1)], axis=3)
    w_v = heads(w[:, 2], 2)
    w_o = np.asarray(inputs["L0_attn_out_w"]).reshape(PAIRS, 2, D, HID).transpose(0, 2, 1, 3)
    b_qkv = np.asarray(inputs["L0_attn_qkv_b"]).reshape(3, HEADS, D).transpose(2, 1, 0)

    whole = (FT - 1) * P
    idx = np.full((P, WF), LUT, np.int32)
    tiles = idx[:, :DOWN_AT - KT * P].reshape(P, FT - 1, 2, KT, P)
    rest = idx[:, DOWN_AT - KT * P:DOWN_AT].reshape(P, KT, P)
    for which, name in enumerate(("gate", "up")):
        rows = np.asarray(inputs[f"L0_ffn_{name}_idx"])
        tiles[:, :, which] = rows[:whole].reshape(FT - 1, P, KT, P).transpose(3, 0, 2, 1)
        rest[:, :, which * UP_AT:which * UP_AT + REST] = rows[whole:].reshape(REST, KT, P).transpose(2, 1, 0)
    down = np.asarray(inputs["L0_ffn_down_idx"]).T
    to = idx[:, DOWN_AT:].reshape(P, FT, HID)
    to[:, :FT - 1] = down[:whole].reshape(FT - 1, P, HID).transpose(1, 0, 2)
    to[:REST, FT - 1] = down[whole:]
    arrays = {
        "x": np.asarray(inputs["L0_attn_x"]).reshape(S, HID), "w_qk": w_qk, "w_v": w_v, "w_o": w_o,
        "b_qkv": b_qkv, "b_out": np.asarray(inputs["L0_attn_out_b"]),
        "lut": np.asarray(inputs["L0_ffn_lut"]), "idx": idx,
    }
    arrays = {name: np.ascontiguousarray(a) for name, a in arrays.items()}
    nc = bacc.Bacc("TRN2", target_bir_lowering=False, num_devices=1)
    args = [nc.dram_tensor(name, a.shape, mybir.dt.from_np(a.dtype), kind="ExternalInput").ap()
            for name, a in arrays.items()]
    out = nc.dram_tensor("out", (S, HID), F32, kind="ExternalOutput").ap()
    block_ffn(nc, *args, out)
    r = run_bass_kernel_spmd(nc, [arrays], core_ids=[0])
    return r.results[0]["out"].reshape(1, S, HID)
```
